# Optimizing a Trainium2 kernel written in Bass

```python
import numpy as np
import jax
import jax.numpy as jnp

def _softmax(x, axis=-1):
    return jax.nn.softmax(x, axis=axis)

def _gelu(x):
    return jax.nn.gelu(x, approximate=True)

def _silu(x):
    return jax.nn.silu(x)

def _sigmoid(x):
    return jax.nn.sigmoid(x)

def _layernorm(x, axis=-1, eps=1e-05):
    m = jnp.mean(x, axis=axis, keepdims=True)
    v = jnp.var(x, axis=axis, keepdims=True)
    return (x - m) / jnp.sqrt(v + eps)

def _scatter_add(tgt, idx, src, axis=0):
    return tgt.at[idx].add(src)

def _segment_sum(src, seg, n):
    return jax.ops.segment_sum(src, seg, n)
kernel_name = 'mk_seq_postln_d2_jaxref_r8_2844fe'

def setup_inputs(seed: int=0):
    np.random.seed(seed)
    _w = jnp.asarray

    def _L0_attn_setup():
        import jax, jax.numpy as jnp
        import numpy as np
        EMBED_DIM = 128
        NUM_HEADS = 16
        HEAD_DIM = EMBED_DIM // NUM_HEADS
        WINDOW_SIZE = 32
        HALF_BAND = 2 * WINDOW_SIZE
        BAND = 2 * HALF_BAND + 1
        key = jax.random.key(seed)
        ks = jax.random.split(key, 9)
        B, T, E = (1, 128, EMBED_DIM)
        scale = 0.02
        return {'hidden_states': jax.random.normal(ks[0], (B, T, E), jnp.float32), 'Wq': jax.random.normal(ks[1], (E, E), jnp.float32) * scale, 'bq': jax.random.normal(ks[2], (E,), jnp.float32) * scale, 'Wk': jax.random.normal(ks[3], (E, E), jnp.float32) * scale, 'bk': jax.random.normal(ks[4], (E,), jnp.float32) * scale, 'Wv': jax.random.normal(ks[5], (E, E), jnp.float32) * scale, 'bv': jax.random.normal(ks[6], (E,), jnp.float32) * scale, 'Wo': jax.random.normal(ks[7], (E, E), jnp.float32) * scale, 'bo': jax.random.normal(ks[8], (E,), jnp.float32) * scale}
    _L0_attn_in = _L0_attn_setup()

    def _L0_ffn_setup():
        import jax, jax.numpy as jnp
        import numpy as np
        D = 128
        E = 12
        HS = 2 * D
        HR = 3 * D
        TAU = 1.5

        def _geglu(h):
            a, g = jnp.split(h, 2, axis=-1)
            return a * jax.nn.gelu(g, approximate=False)
        key = jax.random.key(seed)
        ks = jax.random.split(key, 12)

        def xavier(k, shape):
            fan_in, fan_out = (shape[-2], shape[-1])
            lim = jnp.sqrt(6.0 / (fan_in + fan_out))
            return jax.random.uniform(k, shape, jnp.float32, -lim, lim)
        x = jax.random.normal(ks[0], (2, 128, D), jnp.float32)
        Ws1 = xavier(ks[1], (D, 2 * HS))
        bs1 = jnp.zeros((2 * HS,), jnp.float32)
        Ws2 = xavier(ks[2], (HS, D))
        bs2 = jnp.zeros((D,), jnp.float32)
        We1 = xavier(ks[3], (E, D, 2 * HR))
        be1 = jnp.zeros((E, 2 * HR), jnp.float32)
        We2 = xavier(ks[4], (E, HR, D))
        be2 = jnp.zeros((E, D), jnp.float32)
        Wr = xavier(ks[5], (D, E))
        br = jnp.zeros((E,), jnp.float32)
        return {'x': x, 'Ws1': Ws1, 'bs1': bs1, 'Ws2': Ws2, 'bs2': bs2, 'We1': We1, 'be1': be1, 'We2': We2, 'be2': be2, 'Wr': Wr, 'br': br}
    _L0_ffn_in = _L0_ffn_setup()

    def _L1_attn_setup():
        import jax, jax.numpy as jnp
        import numpy as np
        from jax import lax
        D_MODEL = 128
        D_STATE = 64
        EXPAND = 2
        HEADDIM = 64
        D_INNER = EXPAND * D_MODEL
        NH = D_INNER // HEADDIM
        N_ANG = D_STATE // 2
        A_FLOOR = 0.0001
        BATCH, SEQ = (2, 64)
        D_IN_PROJ = D_INNER + D_INNER + D_STATE + D_STATE + NH + NH + NH + N_ANG

        def _layernorm(x, g, b, eps=1e-05):
            m = x.mean(-1, keepdims=True)
            v = ((x - m) ** 2).mean(-1, keepdims=True)
            return (x - m) / jnp.sqrt(v + eps) * g + b

        def _rope_pairs(v, ang):
            ve, vo = (v[..., 0::2], v[..., 1::2])
            c, s = (jnp.cos(ang), jnp.sin(ang))
            re = ve * c - vo * s
            ro = ve * s + vo * c
            return jnp.stack([re, ro], axis=-1).reshape(v.shape)
        key = jax.random.key(seed)
        ks = jax.random.split(key, 9)
        u = jax.random.normal(ks[0], (BATCH, SEQ, D_MODEL), jnp.float32)
        W_in = jax.random.normal(ks[1], (D_MODEL, D_IN_PROJ), jnp.float32) * 0.02
        W_out = jax.random.normal(ks[2], (D_INNER, D_MODEL), jnp.float32) * 0.02
        dt_bias = jax.random.normal(ks[3], (NH,), jnp.float32) * 0.1
        D_param = jnp.ones((NH,), jnp.float32)
        Bn_g = 1.0 + 0.1 * jax.random.normal(ks[4], (D_STATE,), jnp.float32)
        Bn_b = 0.1 * jax.random.normal(ks[5], (D_STATE,), jnp.float32)
        Cn_g = 1.0 + 0.1 * jax.random.normal(ks[6], (D_STATE,), jnp.float32)
        Cn_b = 0.1 * jax.random.normal(ks[7], (D_STATE,), jnp.float32)
        return {'u': u, 'W_in': W_in, 'W_out': W_out, 'dt_bias': dt_bias, 'D_param': D_param, 'Bn_g': Bn_g, 'Bn_b': Bn_b, 'Cn_g': Cn_g, 'Cn_b': Cn_b}
    _L1_attn_in = _L1_attn_setup()

    def _L1_ffn_setup():
        import jax, jax.numpy as jnp
        import numpy as np
        D_MODEL = 128
        D_FF = 512
        N_EXPERTS = 8
        TOP_K = 2
        LN_EPS = 1e-06

        def _moe(x, router_w, w1, b1, w2, b2, gamma, beta):
            B, S, D = x.shape
            x_flat = x.reshape(-1, D)
            N = x_flat.shape[0]
            logits = x_flat @ router_w
            gate_vals, gate_idx = jax.lax.top_k(logits, TOP_K)
            gate_w = jax.nn.softmax(gate_vals, axis=-1)
            gates = jnp.zeros_like(logits).at[jnp.arange(N)[:, None], gate_idx].set(gate_w)
            h = jax.nn.gelu(jnp.einsum('nd,edf->enf', x_flat, w1) + b1[:, None, :], approximate=False)
            out = jnp.einsum('enf,efd->end', h, w2) + b2[:, None, :]
            res = x_flat[None, :, :] + out
            mu = jnp.mean(res, axis=-1, keepdims=True)
            var = jnp.mean(jnp.square(res - mu), axis=-1, keepdims=True)
            normed = (res - mu) * jax.lax.rsqrt(var + LN_EPS)
            expert_out = normed * gamma[:, None, :] + beta[:, None, :]
            y = jnp.einsum('end,ne->nd', expert_out, gates)
            return y.reshape(B, S, D)
        key = jax.random.key(seed)
        ks = jax.random.split(key, 8)
        x = jax.random.normal(ks[0], (2, 256, D_MODEL), dtype=jnp.float32)
        router_w = jax.random.normal(ks[1], (D_MODEL, N_EXPERTS), dtype=jnp.float32) * 0.02
        w1 = jax.random.normal(ks[2], (N_EXPERTS, D_MODEL, D_FF), dtype=jnp.float32) * 0.02
        b1 = jnp.zeros((N_EXPERTS, D_FF), dtype=jnp.float32)
        w2 = jax.random.normal(ks[3], (N_EXPERTS, D_FF, D_MODEL), dtype=jnp.float32) * 0.02
        b2 = jnp.zeros((N_EXPERTS, D_MODEL), dtype=jnp.float32)
        gamma = jnp.ones((N_EXPERTS, D_MODEL), dtype=jnp.float32)
        beta = jnp.zeros((N_EXPERTS, D_MODEL), dtype=jnp.float32)
        return {'x': x, 'router_w': router_w, 'w1': w1, 'b1': b1, 'w2': w2, 'b2': b2, 'gamma': gamma, 'beta': beta}
    _L1_ffn_in = _L1_ffn_setup()
    _d = {'L0_attn_hidden_states': _L0_attn_in['hidden_states'], 'L0_attn_Wq': _L0_attn_in['Wq'], 'L0_attn_bq': _L0_attn_in['bq'], 'L0_attn_Wk': _L0_attn_in['Wk'], 'L0_attn_bk': _L0_attn_in['bk'], 'L0_attn_Wv': _L0_attn_in['Wv'], 'L0_attn_bv': _L0_attn_in['bv'], 'L0_attn_Wo': _L0_attn_in['Wo'], 'L0_attn_bo': _L0_attn_in['bo'], 'L0_ffn_Ws1': _L0_ffn_in['Ws1'], 'L0_ffn_bs1': _L0_ffn_in['bs1'], 'L0_ffn_Ws2': _L0_ffn_in['Ws2'], 'L0_ffn_bs2': _L0_ffn_in['bs2'], 'L0_ffn_We1': _L0_ffn_in['We1'], 'L0_ffn_be1': _L0_ffn_in['be1'], 'L0_ffn_We2': _L0_ffn_in['We2'], 'L0_ffn_be2': _L0_ffn_in['be2'], 'L0_ffn_Wr': _L0_ffn_in['Wr'], 'L0_ffn_br': _L0_ffn_in['br'], 'L1_attn_W_in': _L1_attn_in['W_in'], 'L1_attn_W_out': _L1_attn_in['W_out'], 'L1_attn_dt_bias': _L1_attn_in['dt_bias'], 'L1_attn_D_param': _L1_attn_in['D_param'], 'L1_attn_Bn_g': _L1_attn_in['Bn_g'], 'L1_attn_Bn_b': _L1_attn_in['Bn_b'], 'L1_attn_Cn_g': _L1_attn_in['Cn_g'], 'L1_attn_Cn_b': _L1_attn_in['Cn_b'], 'L1_ffn_router_w': _L1_ffn_in['router_w'], 'L1_ffn_w1': _L1_ffn_in['w1'], 'L1_ffn_b1': _L1_ffn_in['b1'], 'L1_ffn_w2': _L1_ffn_in['w2'], 'L1_ffn_b2': _L1_ffn_in['b2'], 'L1_ffn_gamma': _L1_ffn_in['gamma'], 'L1_ffn_beta': _L1_ffn_in['beta']}
    _x0 = _d['L0_attn_hidden_states']
    _d['L0_attn_hidden_states'] = jax.random.normal(jax.random.fold_in(jax.random.key(seed), 1), (4, 512, 128), dtype=_x0.dtype)
    del _x0
    return _d

def reference(L0_attn_hidden_states, L0_attn_Wq, L0_attn_bq, L0_attn_Wk, L0_attn_bk, L0_attn_Wv, L0_attn_bv, L0_attn_Wo, L0_attn_bo, L0_ffn_Ws1, L0_ffn_bs1, L0_ffn_Ws2, L0_ffn_bs2, L0_ffn_We1, L0_ffn_be1, L0_ffn_We2, L0_ffn_be2, L0_ffn_Wr, L0_ffn_br, L1_attn_W_in, L1_attn_W_out, L1_attn_dt_bias, L1_attn_D_param, L1_attn_Bn_g, L1_attn_Bn_b, L1_attn_Cn_g, L1_attn_Cn_b, L1_ffn_router_w, L1_ffn_w1, L1_ffn_b1, L1_ffn_w2, L1_ffn_b2, L1_ffn_gamma, L1_ffn_beta):

    def _L0_attn_ref(hidden_states, Wq, bq, Wk, bk, Wv, bv, Wo, bo):
        import jax, jax.numpy as jnp
        import numpy as np
        EMBED_DIM = 128
        NUM_HEADS = 16
        HEAD_DIM = EMBED_DIM // NUM_HEADS
        WINDOW_SIZE = 32
        HALF_BAND = 2 * WINDOW_SIZE
        BAND = 2 * HALF_BAND + 1
        B, T, E = hidden_states.shape
        H, D = (NUM_HEADS, HEAD_DIM)
        S = T
        q = hidden_states @ Wq.T + bq
        k = hidden_states @ Wk.T + bk
        v = hidden_states @ Wv.T + bv
        q = q.reshape(B, T, H, D).transpose(0, 2, 1, 3)
        k = k.reshape(B, S, H, D).transpose(0, 2, 1, 3)
        v = v.reshape(B, S, H, D).transpose(0, 2, 1, 3)
        offsets = jnp.arange(-HALF_BAND, HALF_BAND + 1)
        idx = jnp.arange(T)[:, None] + offsets[None, :]
        valid = (idx >= 0) & (idx < S)
        idxc = jnp.clip(idx, 0, S - 1)
        kb = k[:, :, idxc, :]
        vb = v[:, :, idxc, :]
        scaling = jnp.sqrt(jnp.asarray(D, jnp.float32))
        scores = jnp.einsum('bhtd,bhtwd->bhtw', q, kb) / scaling
        scores = jnp.where(valid[None, None], scores, -jnp.inf)
        probs = jax.nn.softmax(scores, axis=-1)
        ctx = jnp.einsum('bhtw,bhtwd->bhtd', probs, vb)
        ctx = ctx.transpose(0, 2, 1, 3).reshape(B, T, H * D)
        attn_output = ctx @ Wo.T + bo
        return attn_output

    def _L0_ffn_ref(x, Ws1, bs1, Ws2, bs2, We1, be1, We2, be2, Wr, br):
        import jax, jax.numpy as jnp
        import numpy as np
        D = 128
        E = 12
        HS = 2 * D
        HR = 3 * D
        TAU = 1.5

        def _geglu(h):
            a, g = jnp.split(h, 2, axis=-1)
            return a * jax.nn.gelu(g, approximate=False)
        B, T, Dm = x.shape
        xf = x.reshape(-1, Dm)
        ys = _geglu(xf @ Ws1 + bs1) @ Ws2 + bs2
        logits = (xf @ Wr + br) / TAU
        top_val, top_idx = jax.lax.top_k(logits, 2)
        top_w = jax.nn.softmax(top_val, axis=-1)
        onehot = jax.nn.one_hot(top_idx, E, dtype=x.dtype)
        w = jnp.einsum('nke,nk->ne', onehot, top_w)
        h = jnp.einsum('nd,edh->enh', xf, We1) + be1[:, None, :]
        act = _geglu(h)
        yE = jnp.einsum('enh,ehd->end', act, We2) + be2[:, None, :]
        yr = jnp.einsum('end,ne->nd', yE, w)
        return (ys + yr).reshape(B, T, Dm)

    def _L1_attn_ref(u, W_in, W_out, dt_bias, D_param, Bn_g, Bn_b, Cn_g, Cn_b):
        import jax, jax.numpy as jnp
        import numpy as np
        from jax import lax
        D_MODEL = 128
        D_STATE = 64
        EXPAND = 2
        HEADDIM = 64
        D_INNER = EXPAND * D_MODEL
        NH = D_INNER // HEADDIM
        N_ANG = D_STATE // 2
        A_FLOOR = 0.0001
        BATCH, SEQ = (2, 64)
        D_IN_PROJ = D_INNER + D_INNER + D_STATE + D_STATE + NH + NH + NH + N_ANG

        def _layernorm(x, g, b, eps=1e-05):
            m = x.mean(-1, keepdims=True)
            v = ((x - m) ** 2).mean(-1, keepdims=True)
            return (x - m) / jnp.sqrt(v + eps) * g + b

        def _rope_pairs(v, ang):
            ve, vo = (v[..., 0::2], v[..., 1::2])
            c, s = (jnp.cos(ang), jnp.sin(ang))
            re = ve * c - vo * s
            ro = ve * s + vo * c
            return jnp.stack([re, ro], axis=-1).reshape(v.shape)
        B_, L, _ = u.shape
        proj = u @ W_in
        idx = np.cumsum([D_INNER, D_INNER, D_STATE, D_STATE, NH, NH, NH])
        z, x, Bp, Cp, dd_dt, dd_A, trap_raw, angles = jnp.split(proj, idx, axis=-1)
        x4 = x.reshape(B_, L, NH, HEADDIM)
        z4 = z.reshape(B_, L, NH, HEADDIM)
        Bp = _layernorm(Bp, Bn_g, Bn_b)
        Cp = _layernorm(Cp, Cn_g, Cn_b)
        DT = jax.nn.softplus(dd_dt + dt_bias)
        DT_mean = DT.mean(axis=-1, keepdims=True)
        phase = jnp.cumsum(angles * DT_mean, axis=1)
        Bp_rot = _rope_pairs(Bp, phase)
        Cp_rot = _rope_pairs(Cp, phase)
        A = jnp.minimum(-jax.nn.softplus(dd_A), -A_FLOOR)
        decay = jnp.exp(A * DT)
        trap = jax.nn.sigmoid(trap_raw)
        Bx = jnp.einsum('blhp,bln->blhpn', x4, Bp_rot)
        Bx_prev = jnp.pad(Bx[:, :-1], ((0, 0), (1, 0), (0, 0), (0, 0), (0, 0)))
        te = trap[..., None, None]
        inp = (te * Bx + (1.0 - te) * Bx_prev) * DT[..., None, None]
        decay_t = jnp.moveaxis(decay, 1, 0)
        inp_t = jnp.moveaxis(inp, 1, 0)
        C_t = jnp.moveaxis(Cp_rot, 1, 0)

        def step(h, xs):
            d, ip, c = xs
            h = d[:, :, None, None] * h + ip
            y = jnp.einsum('bhpn,bn->bhp', h, c)
            return (h, y)
        h0 = jnp.zeros((B_, NH, HEADDIM, D_STATE), u.dtype)
        _, ys = lax.scan(step, h0, (decay_t, inp_t, C_t))
        y = jnp.moveaxis(ys, 0, 1)
        y = (y + D_param[None, None, :, None] * x4) * jax.nn.silu(z4)
        out = y.reshape(B_, L, D_INNER) @ W_out
        return out

    def _L1_ffn_ref(x, router_w, w1, b1, w2, b2, gamma, beta):
        import jax, jax.numpy as jnp
        import numpy as np
        D_MODEL = 128
        D_FF = 512
        N_EXPERTS = 8
        TOP_K = 2
        LN_EPS = 1e-06

        def _moe(x, router_w, w1, b1, w2, b2, gamma, beta):
            B, S, D = x.shape
            x_flat = x.reshape(-1, D)
            N = x_flat.shape[0]
            logits = x_flat @ router_w
            gate_vals, gate_idx = jax.lax.top_k(logits, TOP_K)
            gate_w = jax.nn.softmax(gate_vals, axis=-1)
            gates = jnp.zeros_like(logits).at[jnp.arange(N)[:, None], gate_idx].set(gate_w)
            h = jax.nn.gelu(jnp.einsum('nd,edf->enf', x_flat, w1) + b1[:, None, :], approximate=False)
            out = jnp.einsum('enf,efd->end', h, w2) + b2[:, None, :]
            res = x_flat[None, :, :] + out
            mu = jnp.mean(res, axis=-1, keepdims=True)
            var = jnp.mean(jnp.square(res - mu), axis=-1, keepdims=True)
            normed = (res - mu) * jax.lax.rsqrt(var + LN_EPS)
            expert_out = normed * gamma[:, None, :] + beta[:, None, :]
            y = jnp.einsum('end,ne->nd', expert_out, gates)
            return y.reshape(B, S, D)
        return _moe(x, router_w, w1, b1, w2, b2, gamma, beta)
    x = L0_attn_hidden_states
    x = _layernorm(x + _L0_attn_ref(x, L0_attn_Wq, L0_attn_bq, L0_attn_Wk, L0_attn_bk, L0_attn_Wv, L0_attn_bv, L0_attn_Wo, L0_attn_bo), axis=-1)
    x = _layernorm(x + _L0_ffn_ref(x, L0_ffn_Ws1, L0_ffn_bs1, L0_ffn_Ws2, L0_ffn_bs2, L0_ffn_We1, L0_ffn_be1, L0_ffn_We2, L0_ffn_be2, L0_ffn_Wr, L0_ffn_br), axis=-1)
    x = _layernorm(x + _L1_attn_ref(x, L1_attn_W_in, L1_attn_W_out, L1_attn_dt_bias, L1_attn_D_param, L1_attn_Bn_g, L1_attn_Bn_b, L1_attn_Cn_g, L1_attn_Cn_b), axis=-1)
    x = _layernorm(x + _L1_ffn_ref(x, L1_ffn_router_w, L1_ffn_w1, L1_ffn_b1, L1_ffn_w2, L1_ffn_b2, L1_ffn_gamma, L1_ffn_beta), axis=-1)
    return x

_drawn_inputs = setup_inputs


def setup_inputs(seed=0):
    import zlib

    import numpy as np

    out = dict(_drawn_inputs(seed))
    spreads = {'L0_ffn_bs1': (0.0, 0.1),
     'L0_ffn_bs2': (0.0, 0.1),
     'L0_ffn_be1': (0.0, 0.1),
     'L0_ffn_be2': (0.0, 0.1),
     'L0_ffn_br': (0.0, 0.1),
     'L1_attn_D_param': (1.0, 0.6),
     'L1_ffn_b1': (0.0, 0.8),
     'L1_ffn_b2': (0.0, 0.1),
     'L1_ffn_gamma': (1.0, 0.2),
     'L1_ffn_beta': (0.0, 0.1)}
    factors = {'L0_attn_Wq': 8.0,
     'L0_attn_bq': 8.0,
     'L0_attn_Wk': 8.0,
     'L0_attn_bk': 8.0,
     'L0_attn_Wv': 5.112,
     'L0_attn_bv': 4.593,
     'L0_attn_Wo': 3.964,
     'L1_attn_dt_bias': 7.437,
     'L1_attn_Bn_g': 8.0,
     'L1_attn_Bn_b': 6.736,
     'L1_attn_Cn_g': 6.15,
     'L1_attn_Cn_b': 7.091,
     'L1_ffn_w1': 2.979,
     'L1_ffn_w2': 2.68}
    for name, (base, spread) in spreads.items():
        noise = np.random.default_rng([zlib.crc32(name.encode()), seed]).standard_normal(out[name].shape)
        drawn = base * np.exp(spread * noise) if base else spread * noise
        out[name] = jnp.asarray(drawn.astype(out[name].dtype))
    for name, factor in factors.items():
        out[name] = (out[name] * factor).astype(out[name].dtype)
    return out
```

```python
import concourse.bass as bass
from concourse import mybir
from contextlib import ExitStack
import math

FP32 = mybir.dt.float32
BF16 = mybir.dt.bfloat16
I32 = mybir.dt.int32
ALU = mybir.AluOpType
ACT = mybir.ActivationFunctionType
AX = mybir.AxisListType.X

P = 128
D = 128
BATCH, SEQ = 4, 512
TOK = BATCH * SEQ
TILES = TOK // P
TPB = SEQ // P
HEADS, HD = 16, 8
HALF = 64
MASKED = -1.0e30
Q_PARTS = [0, 0, 0, 1, 1, 2]
K_PARTS = [0, 1, 2, 0, 1, 0]
QK_ROWS = HD * len(Q_PARTS)
MAX_PARTS = 3
ROUND_MAGIC = 12582912.0


class Semaphores:

    def __init__(self, nc):
        self.nc, self.all = nc, []

    def new(self, name):
        self.all.append(self.nc.alloc_semaphore(name=name))
        return self.all[-1]

    def close(self):
        self.nc.clear_and_free_semaphores(self.all)
        self.nc.all_engine_barrier()


class Signal:

    def __init__(self, ctx, nc, name):
        self.sem = ctx.new(name)
        self.n = 0

    def __call__(self, ins):
        ins.then_inc(self.sem, 1)
        self.n += 1
        return self.n


class Chain:

    def __init__(self, ctx, nc, eng, name):
        self.eng, self.sem, self.n = eng, ctx.new(name), 0

    def __call__(self, ins):
        ins.then_inc(self.sem, 1)
        self.n += 1
        self.eng.wait_ge(self.sem, self.n)

    def loose(self, ins):
        ins.then_inc(self.sem, 1)
        self.n += 1

    def settle(self):
        self.eng.wait_ge(self.sem, self.n)


def bcast_mid(ap, n):
    return ap.unsqueeze(1).to_broadcast([ap.shape[0], n, ap.shape[1]])


def bcast_last(ap, n):
    return ap.unsqueeze(2).to_broadcast([ap.shape[0], ap.shape[1], n])


def make_constants(nc, m, ctx):
    done = Signal(ctx, nc, "constants_done")
    filled = Signal(ctx, nc, "constants_filled")
    with nc.Block() as block:
        @block.gpsimd
        def _(pool):
            g = nc.gpsimd
            for t, v in ((m["ident"], 0.0), (m["identb"], 0.0), (m["tri"], 1.0), (m["tri_strict"], 1.0), (m["ones"], 1.0)):
                filled(g.memset(t[:, :], v))
            filled(g.memset(m["band"][:, :, :], 0.0))
            filled(g.memset(m["causal"][:, :, :], 0.0))
            filled(g.memset(m["ones3"][:, :], 1.0))
            filled(g.memset(m["zeros"][:, :], 0.0))
            filled(g.memset(m["inner"][:, :], 1.0))
            filled(g.iota(m["iota_e"][:, :, :], pattern=[[0, TILES], [1, 12]], base=0, channel_multiplier=0,
                          allow_small_or_imprecise_dtypes=True))
            filled(g.iota(m["iota_j"][:, :], pattern=[[1, m["iota_j"].shape[1]]], base=0, channel_multiplier=0,
                          allow_small_or_imprecise_dtypes=True))
            pool.wait_ge(filled.sem, filled.n)

            def select(t, pattern, base, mult, fill, op=ALU.is_ge):
                done(g.affine_select(out=t, in_=t, compare_op=op, fill=fill, base=base, pattern=pattern,
                                     channel_multiplier=mult))
                pool.wait_ge(done.sem, done.n)

            select(m["ident"][:, :], [[-1, P]], 0, 1, 1.0, ALU.not_equal)
            select(m["identb"][:, :], [[-1, P]], 0, 1, 1.0, ALU.not_equal)
            select(m["tri"][:, :], [[1, P]], 0, -1, 0.0)
            select(m["tri_strict"][:, :], [[1, P]], -1, -1, 0.0)
            select(m["band"][:, :, :], [[0, 2], [1, 256]], 0, -1, MASKED)
            select(m["band"][:, :, :], [[0, 2], [-1, 256]], P, 1, MASKED)
            select(m["causal"][:, :, :], [[0, 4], [1, P]], 0, -1, MASKED)
            inner = m["inner"][:, :].rearrange("p (b c) -> p b c", b=BATCH)
            select(inner, [[0, BATCH], [1, TPB]], 0, 1, 0.0, ALU.not_equal)


def stage_load(nc, m, ctx, A):
    sem = ctx.new("loads")
    with nc.Block() as block:
        @block.sync
        def _(sp):
            n = 0

            def load(dst, src):
                nonlocal n
                sp.dma_start(dst, src).then_inc(sem, 16)
                n += 1

            load(m["X"][:, :, :], A["L0_attn_hidden_states"].rearrange("b (c p) d -> p (b c) d", p=P))
            for i, w in enumerate(("Wq", "Wk", "Wv", "Wo")):
                load(m["Wraw"][:, i * D:(i + 1) * D], A["L0_attn_" + w])
            load(m["bqk"][:, 0:1], A["L0_attn_bq"].rearrange("(p o) -> p o", o=1))
            load(m["bqk"][:, 1:2], A["L0_attn_bk"].rearrange("(p o) -> p o", o=1))

            def row(dst, src):
                load(dst, src.rearrange("(o n) -> o n", o=1).to_broadcast([P, src.shape[0]]))

            row(m["bv"][:, :], A["L0_attn_bv"])
            row(m["bo"][:, :], A["L0_attn_bo"])
            row(m["br"][:, :], A["L0_ffn_br"])
            row(m["bs2"][:, :], A["L0_ffn_bs2"])
            load(m["Wr0"][:, :], A["L0_ffn_Wr"])
            load(m["Ws1"][:, :], A["L0_ffn_Ws1"])
            load(m["Ws2"][:, :, :], A["L0_ffn_Ws2"].rearrange("(c p) d -> p c d", p=P))
            for c in range(4):
                load(m["bs1"][:, c:c + 1], A["L0_ffn_bs1"][c * P:(c + 1) * P].rearrange("(p o) -> p o", o=1))
            load(m["We1"][:, :, :], A["L0_ffn_We1"].rearrange("e p h -> p e h"))
            load(m["We2"][:, :, :], A["L0_ffn_We2"].rearrange("e (c p) d -> p (e c) d", p=P))
            for xs in m["xs"]:
                nt = xs.shape[0] // P
                load(xs.rearrange("(n p) d -> p n d", p=P), bcast_mid(m["zeros"][:, 0:D], nt))
            sp.wait_ge(sem, 16 * n)


def stage_bias(nc, m, ctx, l, b_up, b_down):
    loaded = ctx.new(f"bias{l}_loaded")
    moved = ctx.new(f"bias{l}_moved")
    split = Signal(ctx, nc, f"bias{l}_split")
    with nc.Block() as block:
        @block.vector
        def _(dve):
            v = nc.vector
            link = Chain(ctx, nc, dve, f"bias{l}_chain")
            dve.wait_ge(loaded, 32)
            for k in range(3):
                if k:
                    link(v.tensor_tensor(m["be"][:, :], m["be"][:, :], m["be_parts"][:, k - 1, :], ALU.subtract))
                split(v.tensor_copy(m["be_parts"][:, k, :], m["be"][:, :]))
                dve.wait_ge(split.sem, k + 1)

        @block.sync
        def _(sp):
            up = b_up.shape[1]
            sp.dma_start(m["be"][:, 0:up], b_up).then_inc(loaded, 16)
            sp.dma_start(m["be"][:, up:up + D], b_down).then_inc(loaded, 16)
            for k in range(3):
                sp.wait_ge(split.sem, k + 1)
                sp.dma_start(m["bias3"][l][k:k + 1, :].rearrange("o (e w) -> o e w", e=b_up.shape[0]),
                             m["be_parts"][:, k, :]).then_inc(moved, 16)
            sp.wait_ge(moved, 16 * 3)


def stage_project(nc, m, ctx):
    def sg(name):
        return Signal(ctx, nc, "proj_" + name)

    wT_ps, wT_sb, xT_ps, xT_sb = sg("wT_ps"), sg("wT_sb"), sg("xT_ps"), sg("xT_sb")
    q_ps, k_ps, v_ps = sg("q_ps"), sg("k_ps"), sg("v_ps")
    q_read, k_read, qk_split, v_sb = sg("q_read"), sg("k_read"), sg("qk_split"), sg("v_sb")
    spilled = ctx.new("proj_spilled")
    rep = ctx.new("proj_replicated")
    bank = m["bank"]
    with nc.Block() as block:
        @block.tensor
        def _(pe):
            for i in range(4):
                last = nc.tensor.transpose(bank(7)[:, i * D:(i + 1) * D], m["Wraw"][:, i * D:(i + 1) * D], m["ident"][:, :])
            wT_ps(last)
            for b in range(BATCH):
                if b >= 2:
                    pe.wait_ge(xT_sb.sem, b - 1)
                for c in range(TPB):
                    last = nc.tensor.transpose(bank(b % 2)[:, c * P:(c + 1) * P], m["X"][:, b * TPB + c, :], m["ident"][:, :])
                xT_ps(last)
                if b == 0:
                    pe.wait_ge(wT_sb.sem, 1)
                pe.wait_ge(xT_sb.sem, b + 1)
                xT = m["XT"][:, b * SEQ:(b + 1) * SEQ]
                if b >= 1:
                    pe.wait_ge(q_read.sem, b)
                q_ps(nc.tensor.matmul(bank(2), lhsT=m["WT"][:, 0:D], rhs=xT, start=True, stop=True))
                if b >= 1:
                    pe.wait_ge(k_read.sem, b)
                k_ps(nc.tensor.matmul(bank(3), lhsT=m["WT"][:, D:2 * D], rhs=xT, start=True, stop=True))
                if b >= 1:
                    pe.wait_ge(v_sb.sem, 3 * b)
                for w in range(5):
                    lo, hi = max(0, P * w - HALF), min(SEQ, P * w + HALF)
                    out = (bank(4)[0:HALF, 384:512] if w == 0 else bank(5)[0:HALF, 0:P] if w == 4
                           else bank(4)[:, (w - 1) * P:w * P])
                    last = nc.tensor.matmul(out, lhsT=xT[:, lo:hi], rhs=m["WT"][:, 2 * D:3 * D], start=True, stop=True)
                v_ps(last)

        @block.scalar
        def _(act):
            act.wait_ge(wT_ps.sem, 1)
            wT_sb(nc.scalar.copy(m["WT"][:, :], bank(7)))
            for b in range(BATCH):
                act.wait_ge(xT_ps.sem, b + 1)
                xT_sb(nc.scalar.copy(m["XT"][:, b * SEQ:(b + 1) * SEQ], bank(b % 2)))

        @block.vector
        def _(dve):
            v = nc.vector
            link = Chain(ctx, nc, dve, "proj_chain")
            link(v.memset(m["krep"][:, :, :, :], 1.0))
            link(v.memset(m["Vext"][:, :, :, :], 1.0))
            for b in range(BATCH):
                tok = slice(b * SEQ, (b + 1) * SEQ)
                for i, (ps, read, bk, parts) in enumerate(((q_ps, q_read, 2, m["q3"]), (k_ps, k_read, 3, m["k3"]))):
                    dve.wait_ge(ps.sem, b + 1)
                    if b >= 1:
                        dve.wait_ge(spilled, 16 * 2 * b)
                    link(v.tensor_scalar(parts[:, 0, :], bank(bk), m["bqk"][:, i:i + 1], None, ALU.add))
                    read(v.scalar_tensor_tensor(m["rest"][:, :], bank(bk), m["bqk"][:, i:i + 1], parts[:, 0, :],
                                                ALU.add, ALU.subtract))
                    dve.wait_ge(read.sem, b + 1)
                    link(v.tensor_copy(parts[:, 1, :], m["rest"][:, :]))
                    qk_split(v.tensor_tensor(parts[:, 2, :], m["rest"][:, :], parts[:, 1, :], ALU.subtract))
                    dve.wait_ge(qk_split.sem, 2 * b + i + 1)
                dve.wait_ge(v_ps.sem, b + 1)
                bv = m["bv"][:, :].rearrange("p (h d) -> p h d", h=HEADS)

                def take(dst, src, n):
                    for i in range(n):
                        last = v.tensor_tensor(dst(i), src(i), bv[0:dst(i).shape[0]], ALU.add)
                    v_sb(last)

                def hd(ap):
                    return ap.rearrange("p (h d) -> p h d", h=HEADS)

                take(lambda i: m["Vext"][:, 5 * b + 1 + i, :, 0:HD], lambda i: hd(bank(4)[:, i * P:(i + 1) * P]), 3)
                take(lambda i: m["Vext"][0:HALF, 5 * b, :, 0:HD], lambda i: hd(bank(4)[0:HALF, 384:512]), 1)
                take(lambda i: m["Vext"][0:HALF, 5 * b + 4, :, 0:HD], lambda i: hd(bank(5)[0:HALF, 0:P]), 1)

        @block.sync
        def _(sp):
            for b in range(BATCH):
                for i, parts in enumerate((m["q3"], m["k3"])):
                    sp.wait_ge(qk_split.sem, 2 * b + i + 1)
                    sp.dma_start(m["qk_dram"][i, b].rearrange("k p t -> p k t"), parts[:, :, :]).then_inc(spilled, 16)
                if b < 2:
                    sp.wait_ge(spilled, 32 * (b + 1))
                    replicate(sp, m, b, rep)
            sp.wait_ge(spilled, 32 * BATCH)
            sp.wait_ge(rep, 2 * REP_INC)


REP_DMAS = 2 * len(Q_PARTS) * 2
REP_INC = 16 * REP_DMAS


def replicate(sp, m, b, sem):
    for i, (dst, which) in enumerate(((m["qrep"], Q_PARTS), (m["krep"], K_PARTS))):
        for odd in range(2):
            for r, part in enumerate(which):
                src = m["qk_dram"][i, b, part].rearrange("(g o d) t -> o d g t", o=2, d=HD)[odd]
                p0 = HALF * odd + HD * r
                sp.dma_start(dst[p0:p0 + HD, b % 2, :, :], src).then_inc(sem, 16)


def stage_attention(nc, m, ctx):
    def sg(name):
        return Signal(ctx, nc, "att_" + name)

    s_ps, s_max, mT_ps, m_split = sg("s_ps"), sg("s_max"), sg("mT_ps"), sg("m_split")
    t_ps, exped, masked, o_ps, ctx_sb = sg("t_ps"), sg("exped"), sg("masked"), sg("o_ps"), sg("ctx_sb")
    cT_ps, cT_sb, w_ps, r_sb, t_done = sg("cT_ps"), sg("cT_sb"), sg("w_ps"), sg("r_sb"), sg("t_done")
    placed = ctx.new("att_max_placed")
    rep = ctx.new("att_replicated")
    bank = m["bank"]
    QUADS = HEADS // 4
    units = []
    for b in range(BATCH):
        units += [("max", (b * TPB + j) * QUADS + q) for j in range(TPB) for q in range(QUADS)]
        units += [("prob", (b * 5 + w) * QUADS + q) for w in range(5) for q in range(QUADS)]
    number = {u: i for i, u in enumerate(units)}

    def pair_of_banks(kind, n):
        i = 2 * (number[kind, n] % 3)
        return m["PS"][:, i * 512:(i + 2) * 512].rearrange("p (o g c) -> p o g c", o=2, g=2)

    def slot(h):
        return 4 * (h // 4) + 2 * (h % 2) + h % 4 // 2

    with nc.Block() as block:
        @block.tensor
        def _(pe):
            def free(kind, n):
                i = number[kind, n]
                if i >= 3:
                    last_kind, last_n = units[i - 3]
                    pe.wait_ge((s_max if last_kind == "max" else exped).sem, last_n + 1)

            def maxima(b):
                if b >= 2:
                    pe.wait_ge(rep, REP_INC * (b - 1))
                for j in range(TPB):
                    c0 = HALF if j == 0 else 0
                    c1 = 192 if j == TPB - 1 else 256
                    k0 = P * j - HALF
                    for q in range(QUADS):
                        n = (b * TPB + j) * QUADS + q
                        free("max", n)
                        out = pair_of_banks("max", n)[:, :, :, c0:c1]
                        for o in range(2):
                            nc.tensor.matmul(out[:, o], lhsT=m["identb"][:, :], rhs=m["band"][:, :, c0:c1], start=True, stop=False,
                                             skip_group_check=True)
                        for g in range(2):
                            for o in range(2):
                                rows = slice(HALF * o, HALF * o + QK_ROWS)
                                last = nc.tensor.matmul(out[:, o, g], lhsT=m["qrep"][rows, b % 2, 2 * q + g, j * P:(j + 1) * P],
                                                        rhs=m["krep"][rows, b % 2, 2 * q + g, k0 + c0:k0 + c1],
                                                        start=False, stop=g == 1, skip_group_check=True)
                        s_ps(last)
                    pe.wait_ge(s_max.sem, n + 1)
                    if b * TPB + j >= 1:
                        pe.wait_ge(m_split.sem, b * TPB + j)
                    mT_ps(nc.tensor.transpose(bank(7)[0:HEADS, 384:512], m["mx"][:, (b * TPB + j) * HEADS:(b * TPB + j + 1) * HEADS],
                                              m["ident"][:, :]))

            def scores_t(b, w):
                k0, k1 = max(0, P * w - HALF), min(SEQ, P * w + HALF)
                q0, q1 = max(0, P * (w - 1)), min(SEQ, P * (w + 1))
                c0 = P if w == 0 else 0
                for quad in range(QUADS):
                    n = (b * 5 + w) * QUADS + quad
                    free("prob", n)
                    out = pair_of_banks("prob", n)
                    for g in range(2):
                        for o in range(2):
                            rows = slice(HALF * o, HALF * o + QK_ROWS + MAX_PARTS)
                            last = nc.tensor.matmul(out[0:k1 - k0, o, g, c0:c0 + q1 - q0],
                                                    lhsT=m["krep"][rows, b % 2, 2 * quad + g, k0:k1],
                                                    rhs=m["qrep"][rows, b % 2, 2 * quad + g, q0:q1],
                                                    start=True, stop=True)
                    t_ps(last)

            def values(b, j):
                n = b * TPB + j
                pe.wait_ge(masked.sem, (b * 5 + j + 2) * QUADS)
                if n >= 1:
                    pe.wait_ge(ctx_sb.sem, n)
                for h in range(HEADS):
                    out = bank(6)[:, h * (HD + 1):(h + 1) * (HD + 1)]
                    for i, w in enumerate((j, j + 1)):
                        keys = HALF if w in (0, 4) else P
                        c = P * (1 - i)
                        last = nc.tensor.matmul(out, lhsT=m["PT"][0:keys, (b * 5 + w) % 3, slot(h), c:c + P],
                                                rhs=m["Vext"][0:keys, 5 * b + w, h, :], start=i == 0, stop=i == 1)
                o_ps(last)

            def project(n):
                pe.wait_ge(ctx_sb.sem, n + 1)
                if n >= 1:
                    pe.wait_ge(r_sb.sem, n)
                cT_ps(nc.tensor.transpose(bank(7)[:, 0:P], m["ctx"][:, n % 2, :], m["ident"][:, :]))
                pe.wait_ge(cT_sb.sem, n + 1)
                w_ps(nc.tensor.matmul(bank(7)[:, P:2 * P], lhsT=m["ctxT"][:, :], rhs=m["WT"][:, 3 * D:4 * D], start=True, stop=True))

            for b in range(BATCH):
                maxima(b)
                pe.wait_ge(placed, 16 * 6 * (b + 1))
                for w in range(5):
                    scores_t(b, w)
                    if w >= 2:
                        values(b, w - 2)
                    if w >= 3:
                        project(b * TPB + w - 3)
                values(b, 3)
                for j in (2, 3):
                    project(b * TPB + j)

        @block.vector
        def _(dve):
            v = nc.vector
            link = Chain(ctx, nc, dve, "att_chain")

            def reduce(b):
                for j in range(TPB):
                    c0 = HALF if j == 0 else 0
                    c1 = 192 if j == TPB - 1 else 256
                    for q in range(QUADS):
                        n = (b * TPB + j) * QUADS + q
                        dve.wait_ge(s_ps.sem, n + 1)
                        s_max(v.tensor_reduce(m["mx"][:, 4 * n:4 * n + 4].rearrange("p (g o) -> p o g", o=2),
                                              pair_of_banks("max", n)[:, :, :, c0:c1], AX, ALU.max))
                    dve.wait_ge(mT_ps.sem, b * TPB + j + 1)
                    if b >= 1 and j == 0:
                        dve.wait_ge(placed, 16 * 6 * b)
                    src, tok = bank(7)[0:HEADS, 384:512], slice(j * P, (j + 1) * P)
                    link(v.tensor_scalar(m["m3"][:, 0, tok], src, -1.0, None, ALU.mult))
                    link(v.scalar_tensor_tensor(m["mrest"][:, :], src, -1.0, m["m3"][:, 0, tok], ALU.mult, ALU.subtract))
                    link(v.tensor_copy(m["m3"][:, 1, tok], m["mrest"][:, :]))
                    m_split(v.tensor_tensor(m["m3"][:, 2, tok], m["mrest"][:, :], m["m3"][:, 1, tok], ALU.subtract))

            def normalise(n):
                dve.wait_ge(o_ps.sem, n + 1)
                if n >= 2:
                    dve.wait_ge(cT_ps.sem, n - 1)
                o = bank(6)[:, 0:HEADS * (HD + 1)].rearrange("p (h e) -> p h e", h=HEADS)
                link(v.reciprocal(m["rden"][:, :], o[:, :, HD]))
                ctx_sb(v.tensor_tensor(m["ctx"][:, n % 2, :].rearrange("p (h d) -> p h d", h=HEADS), o[:, :, 0:HD],
                                       bcast_last(m["rden"][:, :], HD), ALU.mult))

            def residual(n):
                dve.wait_ge(w_ps.sem, n + 1)
                link(v.tensor_tensor(m["R"][:, n, :], bank(7)[:, P:2 * P], m["bo"][:, :], ALU.add))
                r_sb(v.tensor_tensor(m["R"][:, n, :], m["R"][:, n, :], m["X"][:, n, :], ALU.add))

            for b in range(BATCH):
                reduce(b)
                for w in range(2, 5):
                    normalise(b * TPB + w - 2)
                    if w >= 3:
                        residual(b * TPB + w - 3)
                normalise(b * TPB + 3)
                for j in (2, 3):
                    residual(b * TPB + j)

        @block.scalar
        def _(act):
            def exps(b, w):
                keys = HALF if w in (0, 4) else P
                c0, c1 = (P if w == 0 else 0), (P if w == 4 else 2 * P)
                n = b * 5 + w
                if n >= 3:
                    pb, pw = divmod(n - 3, 5)
                    act.wait_ge(o_ps.sem, pb * TPB + min(pw + 1, TPB))
                for quad in range(QUADS):
                    g = n * QUADS + quad
                    act.wait_ge(t_ps.sem, g + 1)
                    exped(nc.scalar.activation(m["PT"][0:keys, n % 3, 4 * quad:4 * quad + 4, c0:c1].rearrange("p (o g) c -> p o g c", o=2), pair_of_banks("prob", g)[0:keys, :, :, c0:c1],
                                               ACT.Exp, scale=1.0 / math.sqrt(HD)))

            def ctxT(n):
                act.wait_ge(cT_ps.sem, n + 1)
                cT_sb(nc.scalar.copy(m["ctxT"][:, :], bank(7)[:, 0:P]))

            for b in range(BATCH):
                for w in range(5):
                    exps(b, w)
                    if w >= 3:
                        ctxT(b * TPB + w - 3)
                for j in (2, 3):
                    ctxT(b * TPB + j)

        @block.gpsimd
        def _(pool):
            for b in range(BATCH):
                for w in range(5):
                    keys = HALF if w in (0, 4) else P
                    n = b * 5 + w
                    for quad in range(QUADS):
                        g = n * QUADS + quad
                        pool.wait_ge(exped.sem, g + 1)
                        t = m["PT"][0:keys, n % 3, 4 * quad:4 * quad + 4, :]
                        if w >= 1:
                            last = nc.gpsimd.affine_select(out=t[:, :, 0:P], in_=t[:, :, 0:P], compare_op=ALU.is_ge, fill=0.0,
                                                           base=0, pattern=[[0, 4], [1, P]], channel_multiplier=-1)
                        if w <= 3:
                            last = nc.gpsimd.affine_select(out=t[:, :, P:2 * P], in_=t[:, :, P:2 * P], compare_op=ALU.is_ge,
                                                           fill=0.0, base=HALF if w == 0 else 0,
                                                           pattern=[[0, 4], [-1, P]], channel_multiplier=1)
                        masked(last)

        @block.sync
        def _(sp):
            for b in range(BATCH):
                sp.wait_ge(m_split.sem, TPB * (b + 1))
                for o in range(2):
                    for part in range(MAX_PARTS):
                        p = HALF * o + QK_ROWS + part
                        sp.dma_start(m["qrep"][p:p + 1, b % 2, :, :], m["m3"][o:HEADS:2, part, :]).then_inc(placed, 16)
                if 1 <= b <= 2:
                    sp.wait_ge(o_ps.sem, TPB * b)
                    replicate(sp, m, b + 1, rep)
            sp.wait_ge(placed, 16 * 6 * BATCH)


def stage_layernorm(nc, m, ctx, name, out_dram=None):
    stats, rooted, done, cent = (Signal(ctx, nc, name + s) for s in ("_stats", "_rooted", "_done", "_agg"))
    stored = ctx.new(name + "_stored")
    with nc.Block() as block:
        @block.vector
        def _(dve):
            v = nc.vector
            for n in range(TILES):
                cent(v.bn_stats(m["bn"][:, n, :], m["R"][:, n, :]))
            for n in range(TILES):
                dve.wait_ge(cent.sem, n + 1)
                last = cent(v.bn_aggr(m["mv"][:, n, :], m["bn"][:, n, :]))
            dve.wait_ge(cent.sem, 2 * TILES)
            stats(v.tensor_scalar(m["std"][:, :], m["mv"][:, :, 1], 1e-5, None, ALU.add))
            dve.wait_ge(rooted.sem, 1)
            stats(v.reciprocal(m["rstd"][:, :], m["root"][:, :]))
            dve.wait_ge(stats.sem, 2)
            for n in range(TILES):
                done(v.tensor_scalar(m["X"][:, n, :], m["R"][:, n, :], m["mv"][:, n, 0:1], m["rstd"][:, n:n + 1], ALU.subtract, ALU.mult))

        @block.scalar
        def _(act):
            act.wait_ge(stats.sem, 1)
            rooted(nc.scalar.activation(m["root"][:, :], m["std"][:, :], ACT.Sqrt))

        @block.sync
        def _(sp):
            if out_dram is not None:
                o = out_dram.rearrange("b (c p) d -> p (b c) d", p=P)
                for q in range(4):
                    sp.wait_ge(done.sem, 4 * (q + 1))
                    sp.dma_start(o[:, 4 * q:4 * q + 4, :], m["X"][:, 4 * q:4 * q + 4, :]).then_inc(stored, 16)
                sp.wait_ge(stored, 64)
            else:
                sp.wait_ge(done.sem, TILES)


def transpose_x(nc, pe, m, x_ps, x_sb, banks):
    for q in range(TILES // 4):
        if q >= 2:
            pe.wait_ge(x_sb.sem, q - 1)
        for c in range(4):
            last = nc.tensor.transpose(m["bank"](banks[q % 2])[:, c * P:(c + 1) * P], m["X"][:, 4 * q + c, :], m["ident"][:, :])
        x_ps(last)


def copy_xt(nc, act, m, x_ps, x_sb, banks):
    for q in range(TILES // 4):
        act.wait_ge(x_ps.sem, q + 1)
        x_sb(nc.scalar.copy(m["XT"][:, q * 512:(q + 1) * 512], m["bank"](banks[q % 2])))


def stage_router(nc, m, ctx, layer, E, tau, NT, Wr, br, shared):
    def sg(name):
        return Signal(ctx, nc, f"route{layer}_" + name)

    x_ps, x_sb, l_ps, picked, c_ps = sg("x_ps"), sg("x_sb"), sg("l_ps"), sg("picked"), sg("c_ps")
    gap, gexp, slots, zz = sg("gap"), sg("gexp"), sg("slots"), sg("zz")
    h_ps, h_act, h_sb, y_ps, y_sb = sg("h_ps"), sg("h_act"), sg("h_sb"), sg("y_ps"), sg("y_sb")
    scattered = ctx.new(f"route{layer}_scattered")
    bank = m["bank"]

    def shared_up(dve, v, q):
        for c in range(2):
            dve.wait_ge(h_act.sem, 2 * q + c + 1)
            dve.wait_ge(h_ps.sem, 4 * q + 3 + c)
            if q >= 1:
                dve.wait_ge(y_ps.sem, q)
            h_sb(v.scalar_tensor_tensor(m["sh_act"][:, c, :], bank(4 + c), m["bs1"][:, c:c + 1], m["sh_gate"][:, c, :],
                                        ALU.add, ALU.mult))

    def v3(t):
        return t[:, 0:TILES * E].rearrange("p (t e) -> p t e", e=E)

    L, EQ, VAL, OH1, OH2, OFF = (v3(t) for t in m["rt"])
    iota_e = m["iota_e"][:, :, 0:E]
    with nc.Block() as block:
        @block.tensor
        def _(pe):
            transpose_x(nc, pe, m, x_ps, x_sb, (0, 1))
            if layer == 1:
                pe.wait_ge(m["load1"], m["load1_n"])
            for n in range(TILES):
                pe.wait_ge(x_sb.sem, n // 4 + 1)
                last = nc.tensor.matmul(bank(2)[:, n * E:(n + 1) * E], lhsT=m["XT"][:, n * P:(n + 1) * P], rhs=Wr[:, :],
                                        start=True, stop=True)
            l_ps(last)

            if not shared:
                pe.wait_ge(picked.sem, 1)
                nc.tensor.matmul(bank(2)[:, 0:TILES * E], lhsT=m["tri_strict"][:, :], rhs=m["rt"][1][:, 0:TILES * E], start=True, stop=True)
                c_ps(nc.tensor.matmul(bank(3)[:, 0:TILES * E], lhsT=m["ones"][:, :], rhs=m["rt"][1][:, 0:TILES * E], start=True, stop=True))
            else:
                for q in range(4):
                    for c in (2, 3, 0, 1):
                        if q >= 1:
                            if c >= 2:
                                pe.wait_ge(h_act.sem, 2 * (q - 1) + c - 1)
                            else:
                                pe.wait_ge(h_sb.sem, 2 * (q - 1) + c + 1)
                        h_ps(nc.tensor.matmul(bank(4 + c), lhsT=m["Ws1"][:, c * P:(c + 1) * P],
                                              rhs=m["XT"][:, q * 512:(q + 1) * 512], start=True, stop=True))
                    if q == 0:
                        pe.wait_ge(picked.sem, 1)
                        nc.tensor.matmul(bank(2)[:, 0:TILES * E], lhsT=m["tri_strict"][:, :], rhs=m["rt"][1][:, 0:TILES * E],
                                         start=True, stop=True)
                        c_ps(nc.tensor.matmul(bank(3)[:, 0:TILES * E], lhsT=m["ones"][:, :], rhs=m["rt"][1][:, 0:TILES * E],
                                              start=True, stop=True))
                    pe.wait_ge(h_sb.sem, 2 * (q + 1))
                    for c in range(4):
                        n = 4 * q + c
                        if n >= 4:
                            pe.wait_ge(y_sb.sem, n // 4)
                        for k in range(2):
                            last = nc.tensor.matmul(bank(q % 2)[:, c * P:(c + 1) * P],
                                                    lhsT=m["sh_act"][:, k, c * P:(c + 1) * P], rhs=m["Ws2"][:, k, :],
                                                    start=k == 0, stop=k == 1)
                    y_ps(last)

        @block.scalar
        def _(act):
            copy_xt(nc, act, m, x_ps, x_sb, (0, 1))
            if shared:
                for q in range(4):
                    for c in (2, 3):
                        act.wait_ge(h_ps.sem, 4 * q + c - 1)
                        if q >= 1:
                            act.wait_ge(h_sb.sem, 2 * (q - 1) + c - 1)
                        h_act(nc.scalar.activation(m["sh_gate"][:, c - 2, :], bank(4 + c), ACT.Gelu, bias=m["bs1"][:, c:c + 1]))
            act.wait_ge(gap.sem, 1)
            gexp(nc.scalar.activation(m["gexp"][:, :], m["gap"][:, :], ACT.Exp, scale=1.0 / tau))

        @block.vector
        def _(dve):
            v = nc.vector
            link = Chain(ctx, nc, dve, f"route{layer}_chain")
            dve.wait_ge(l_ps.sem, 1)
            src = bank(2)[:, 0:TILES * E].rearrange("p (t e) -> p t e", e=E)
            if br is not None:
                link(v.tensor_tensor(L, src, bcast_mid(br[:, :], TILES), ALU.add))
            else:
                link(v.tensor_copy(L, src))
            for k, oh in enumerate((OH1, OH2)):
                top = m["top"][:, k, :]
                link(v.tensor_reduce(top, L, AX, ALU.max))
                link(v.tensor_tensor(EQ, L, bcast_last(top, E), ALU.is_equal))
                link(v.scalar_tensor_tensor(VAL, EQ, -100.0, iota_e, ALU.mult, ALU.add))
                link(v.tensor_reduce(m["first"][:, :], VAL, AX, ALU.min))
                link(v.tensor_tensor(oh, VAL, bcast_last(m["first"][:, :], E), ALU.is_equal))
                if k == 0:
                    link(v.scalar_tensor_tensor(L, OH1, -3.0e38, L, ALU.mult, ALU.add))
            picked(v.tensor_tensor(EQ, OH1, OH2, ALU.add))
            gap(v.tensor_tensor(m["gap"][:, :], m["top"][:, 1, :], m["top"][:, 0, :], ALU.subtract))
            if shared:
                shared_up(dve, v, 0)
            dve.wait_ge(c_ps.sem, 1)
            cum = bank(2)[:, 0:TILES * E].rearrange("p (t e) -> p t e", e=E)
            tot = bank(3)[:, 0:TILES * E].rearrange("p (t e) -> p t e", e=E)
            link(v.memset(OFF[:, 0, :], 0.0))
            for n in range(1, TILES):
                link(v.tensor_tensor(OFF[:, n, :], OFF[:, n - 1, :], tot[:, n - 1, :], ALU.add))
            link(v.tensor_tensor(m["cnt"][:, 0:E], OFF[:, TILES - 1, :], tot[:, TILES - 1, :], ALU.add))
            link(v.tensor_scalar(m["cnt"][:, 0:E], m["cnt"][:, 0:E], (P - 1) / 2.0, 1.0 / P, ALU.add, ALU.mult))
            link(v.tensor_scalar(m["cnt"][:, 0:E], m["cnt"][:, 0:E], ROUND_MAGIC, None, ALU.add))
            link(v.tensor_scalar(m["cnt"][:, 0:E], m["cnt"][:, 0:E], ROUND_MAGIC, None, ALU.subtract))
            link(v.memset(m["start"][:, 0:1], 0.0))
            for e in range(1, E):
                link(v.tensor_tensor(m["start"][:, e:e + 1], m["start"][:, e - 1:e], m["cnt"][:, e - 1:e], ALU.add))
            link(v.tensor_scalar(m["base"][:, 0:E], m["start"][:, 0:E], float(P), None, ALU.mult))
            link(v.tensor_tensor(OFF, OFF, bcast_mid(m["base"][:, 0:E], TILES), ALU.add))
            link(v.tensor_tensor(OFF, OFF, cum, ALU.add))
            for k, oh in enumerate((OH1, OH2)):
                link(v.tensor_tensor(VAL, OFF, oh, ALU.mult))
                link(v.tensor_reduce(m["posf"][:, k, :], VAL, AX, ALU.add))
            slots(v.tensor_copy(m["pos"][:, :, :], m["posf"][:, :, :]))
            cmp = m["cmp"][0:1, 0:NT * E].rearrange("p (j e) -> p j e", e=E)
            link(v.tensor_tensor(cmp, bcast_mid(m["start"][0:1, 0:E], NT), bcast_last(m["iota_j"][0:1, 0:NT], E), ALU.is_le))
            link(v.tensor_reduce(m["eidf"][0:1, 0:NT], cmp, AX, ALU.add))
            link(v.tensor_scalar(m["eidf"][0:1, 0:NT], m["eidf"][0:1, 0:NT], 1.0, None, ALU.subtract))
            link(v.tensor_copy(m["eid"][0:1, 0:NT], m["eidf"][0:1, 0:NT]))
            if layer == 1:
                for k, oh in enumerate((OH1, OH2)):
                    link(v.tensor_tensor(VAL, iota_e, oh, ALU.mult))
                    link(v.tensor_reduce(m["posf"][:, k, :], VAL, AX, ALU.add))
                slots(v.tensor_copy(m["choice"][:, :, :], m["posf"][:, :, :]))
            if shared:
                for q in range(4):
                    if q >= 1:
                        shared_up(dve, v, q)
                    dve.wait_ge(y_ps.sem, q + 1)
                    dst = m["R"][:, 4 * q:4 * q + 4, :]
                    y_sb(v.tensor_tensor(dst, bank(q % 2).rearrange("p (t d) -> p t d", t=4), bcast_mid(m["bs2"][:, :], 4), ALU.add))
                    dve.wait_ge(y_sb.sem, q + 1)
                    link(v.tensor_tensor(dst, dst, m["X"][:, 4 * q:4 * q + 4, :], ALU.add))
            dve.wait_ge(gexp.sem, 1)
            link(v.tensor_scalar(m["w"][:, 0, :], m["gexp"][:, :], 1.0, None, ALU.add))
            link(v.reciprocal(m["w"][:, 0, :], m["w"][:, 0, :]))
            link(v.tensor_tensor(m["w"][:, 1, :], m["w"][:, 0, :], m["gexp"][:, :], ALU.mult))

        @block.gpsimd
        def _(pool):
            pool.wait_ge(slots.sem, 1)
            for n in range(TILES):
                for k in range(2):
                    nc.gpsimd.indirect_dma_start(
                        out=m["xs"][layer][:, :], out_offset=bass.IndirectOffsetOnAxis(ap=m["pos"][:, k, n:n + 1], axis=0),
                        in_=m["X"][:, n, :], in_offset=None).then_inc(scattered, 16)
            pool.wait_ge(scattered, 16 * 2 * TILES)
            if layer == 1:
                pool.wait_ge(slots.sem, 2)


class Tile:

    def __init__(self, c, it=None):
        self.c, self.it = c, it
        self.par = c % 2
        self.v = c if it is None else it * 2 + c
        self.half = c // 2 if it is None else it + c // 2

    def plus(self, k):
        return Tile(self.c + k, self.it)

    def at_least(self, k):
        return self.it is not None or self.c >= k


def walk(eng, NT, step):
    for c in range(3):
        step(Tile(c))
    with eng.Fori(0, (NT - 4) // 2) as it:
        step(Tile(3, it))
        step(Tile(4, it))
    step(Tile(NT - 1))


def stage_experts(nc, m, ctx, layer, NT, HID, W1, W2, bias3, E):
    def sg(name):
        return Signal(ctx, nc, f"exp{layer}_" + name)

    x_ps, x_sb, h_ps, gelu, act_sb = sg("x_ps"), sg("x_sb"), sg("h_ps"), sg("gelu"), sg("act_sb")
    aT_ps, aT_sb, y_ps, y_sb = sg("aT_ps"), sg("aT_sb"), sg("y_ps"), sg("y_sb")
    loaded = [ctx.new(f"exp{layer}_loaded{i}") for i in range(2)]
    stored = [ctx.new(f"exp{layer}_stored{i}") for i in range(2)]
    bank = m["bank"]
    glu = layer == 0
    UP = 2 * HID if glu else HID
    WB = UP + D
    KC = HID // P
    act_done = act_sb if glu else gelu
    w1 = W1[:, :, :].rearrange("p e h -> p (e h)")
    w2 = W2[:, :, :].rearrange("p c d -> p (c d)")

    with nc.Block() as block:
        @block.sync
        def _(sp):
            def load(t):
                if t.at_least(2):
                    sp.wait_ge(x_ps.sem, t.v - 1)
                sp.dma_start(m["xin"][:, t.par, :], m["xs"][layer][bass.ds(t.v * P, P), :]).then_inc(loaded[t.par], 16)

            def store(t):
                sp.wait_ge(y_sb.sem, t.v + 1)
                sp.dma_start(m["ys"][layer][bass.ds(t.v * P, P), :], m["y_sb"][:, t.par, :]).then_inc(stored[t.par], 16)

            load(Tile(0))
            load(Tile(1))
            for c in range(3):
                load(Tile(c + 2))
                store(Tile(c))
            with sp.Fori(0, (NT - 6) // 2) as it:
                for c in (3, 4):
                    load(Tile(c + 2, it))
                    store(Tile(c, it))
            load(Tile(NT - 1))
            for c in (NT - 3, NT - 2, NT - 1):
                store(Tile(c))
            for s in stored:
                sp.wait_ge(s, 16 * (NT // 2))

        @block.tensor
        def _(pe):
            def expert(t):
                return pe.value_load(m["eid"][0:1, bass.ds(t.v, 1)], min_val=0, max_val=E - 1)

            def x_t(t):
                pe.wait_ge(loaded[t.par], (t.half + 1) * 16)
                if t.at_least(1):
                    pe.wait_ge(x_sb.sem, t.v)
                x_ps(nc.tensor.transpose(bank(0)[:, 0:P], m["xin"][:, t.par, :], m["ident"][:, :]))

            def up(t):
                e = expert(t)
                pe.wait_ge(x_sb.sem, t.v + 1)
                if t.at_least(2):
                    pe.wait_ge(act_done.sem, t.v - 1)
                for i in range(UP // HID):
                    out = bank(2 + 2 * i + t.par)[:, 0:HID]
                    nc.tensor.matmul(out, lhsT=m["ones3"][:, :], rhs=bias3[:, bass.ds(e * WB + i * HID, HID)], start=True, stop=False)
                    last = nc.tensor.matmul(out, lhsT=m["xTt"][:, t.par, :], rhs=w1[:, bass.ds(e * UP + i * HID, HID)],
                                            start=False, stop=True)
                h_ps(last)

            def act_t(t):
                pe.wait_ge(act_done.sem, t.v + 1)
                if t.at_least(2):
                    pe.wait_ge(aT_sb.sem, t.v - 1)
                for k in range(KC):
                    last = nc.tensor.transpose(bank(6 + t.par)[:, k * P:(k + 1) * P], m["act_sb"][:, t.par, k * P:(k + 1) * P],
                                               m["ident"][:, :])
                aT_ps(last)

            def down(t):
                e = expert(t)
                pe.wait_ge(aT_sb.sem, t.v + 1)
                if t.at_least(1):
                    pe.wait_ge(y_sb.sem, t.v)
                out = bank(1)[:, 0:P]
                nc.tensor.matmul(out, lhsT=m["ones3"][:, :], rhs=bias3[:, bass.ds(e * WB + UP, D)], start=True, stop=False)
                for k in range(KC):
                    last = nc.tensor.matmul(out, lhsT=m["actT"][:, t.par, k * P:(k + 1) * P],
                                            rhs=w2[:, bass.ds(e * (KC * D) + k * D, D)], start=False, stop=k == KC - 1)
                y_ps(last)

            x_t(Tile(0))

            def step(t):
                if t.at_least(1):
                    act_t(t.plus(-1))
                if t.it is not None or t.c < NT - 1:
                    x_t(t.plus(1))
                up(t)
                if t.at_least(1):
                    down(t.plus(-1))

            walk(pe, NT, step)
            act_t(Tile(NT - 1))
            down(Tile(NT - 1))

        @block.scalar
        def _(act):
            def x_copy(t):
                act.wait_ge(x_ps.sem, t.v + 1)
                if t.at_least(2):
                    act.wait_ge(h_ps.sem, t.v - 1)
                x_sb(nc.scalar.copy(m["xTt"][:, t.par, :], bank(0)[:, 0:P]))

            def activate(t):
                act.wait_ge(h_ps.sem, t.v + 1)
                if glu:
                    if t.at_least(2):
                        act.wait_ge(act_sb.sem, t.v - 1)
                    gelu(nc.scalar.activation(m["gate"][:, t.par, 0:HID], bank(4 + t.par)[:, 0:HID], ACT.Gelu))
                else:
                    if t.at_least(2):
                        act.wait_ge(aT_ps.sem, t.v - 1)
                    gelu(nc.scalar.activation(m["act_sb"][:, t.par, 0:HID], bank(2 + t.par)[:, 0:HID], ACT.Gelu))

            def y_copy(t):
                act.wait_ge(y_ps.sem, t.v + 1)
                if t.at_least(2):
                    act.wait_ge(stored[t.par], t.half * 16)
                y_sb(nc.scalar.copy(m["y_sb"][:, t.par, :], bank(1)[:, 0:P]))

            x_copy(Tile(0))

            def step(t):
                if t.it is not None or t.c < NT - 1:
                    x_copy(t.plus(1))
                activate(t)
                if t.at_least(1):
                    y_copy(t.plus(-1))

            walk(act, NT, step)
            y_copy(Tile(NT - 1))

        @block.vector
        def _(dve):
            v = nc.vector

            def aT_copy(t):
                dve.wait_ge(aT_ps.sem, t.v + 1)
                if t.at_least(2):
                    dve.wait_ge(y_ps.sem, t.v - 1)
                aT_sb(v.tensor_copy(m["actT"][:, t.par, 0:HID], bank(6 + t.par)[:, 0:HID]))

            def multiply(t):
                dve.wait_ge(gelu.sem, t.v + 1)
                if t.at_least(2):
                    dve.wait_ge(aT_ps.sem, t.v - 1)
                act_sb(v.tensor_tensor(m["act_sb"][:, t.par, 0:HID], bank(2 + t.par)[:, 0:HID], m["gate"][:, t.par, 0:HID], ALU.mult))

            def step(t):
                if t.at_least(1):
                    aT_copy(t.plus(-1))
                if glu:
                    multiply(t)

            walk(dve, NT, step)
            aT_copy(Tile(NT - 1))

        if layer == 1:
            gathered = ctx.new("gb_gathered")

            @block.gpsimd
            def _(pool):
                for n in range(TILES):
                    for k in range(2):
                        off = bass.IndirectOffsetOnAxis(ap=m["choice"][:, k, n:n + 1], axis=0)
                        nc.gpsimd.indirect_dma_start(out=m["Gam"][k][:, n, :], out_offset=None, in_=m["gamma_dram"], in_offset=off).then_inc(gathered, 16)
                        nc.gpsimd.indirect_dma_start(out=m["Bet"][k][:, n, :], out_offset=None, in_=m["beta_dram"], in_offset=off).then_inc(gathered, 16)
                pool.wait_ge(gathered, 16 * 4 * TILES)


def stage_combine(nc, m, ctx, layer):
    gathered = [ctx.new(f"comb{layer}_gathered{n}") for n in range(2)]
    added = Signal(ctx, nc, f"comb{layer}_added")
    stats, rooted = Signal(ctx, nc, f"comb{layer}_stats"), Signal(ctx, nc, f"comb{layer}_rooted")
    with nc.Block() as block:
        @block.gpsimd
        def _(pool):
            for n in range(TILES):
                for k in range(2):
                    nc.gpsimd.indirect_dma_start(
                        out=m["G"][k][:, n, :], out_offset=None, in_=m["ys"][layer][:, :],
                        in_offset=bass.IndirectOffsetOnAxis(ap=m["pos"][:, k, n:n + 1], axis=0)).then_inc(gathered[k], 16)

        @block.vector
        def _(dve):
            v = nc.vector
            link = Chain(ctx, nc, dve, f"comb{layer}_chain")
            for k in range(2):
                dve.wait_ge(gathered[k], 16 * TILES)
            if layer == 1:
                for k in range(2):
                    link(v.tensor_tensor(m["G"][k][:, :, :], m["G"][k][:, :, :], m["X"][:, :, :], ALU.add))
                    for n in range(TILES):
                        link.loose(v.bn_stats(m["bn"][:, n, :], m["G"][k][:, n, :]))
                    link.settle()
                    for n in range(TILES):
                        link.loose(v.bn_aggr(m["mv"][:, n, :], m["bn"][:, n, :]))
                    link.settle()
                    stats(v.tensor_scalar(m["std"][:, :], m["mv"][:, :, 1], 1e-6, None, ALU.add))
                    dve.wait_ge(rooted.sem, k + 1)
                    link(v.reciprocal(m["rstd"][:, :], m["root"][:, :]))
                    for n in range(TILES):
                        link.loose(v.tensor_scalar(m["G"][k][:, n, :], m["G"][k][:, n, :], m["mv"][:, n, 0:1], m["rstd"][:, n:n + 1],
                                                   ALU.subtract, ALU.mult))
                    link.settle()
                    link(v.tensor_tensor(m["G"][k][:, :, :], m["G"][k][:, :, :], m["Gam"][k][:, :, :], ALU.mult))
                    link(v.tensor_tensor(m["G"][k][:, :, :], m["G"][k][:, :, :], m["Bet"][k][:, :, :], ALU.add))
            base = m["R"] if layer == 0 else m["X"]
            for n in range(TILES):
                link.loose(v.scalar_tensor_tensor(m["R"][:, n, :], m["G"][0][:, n, :], m["w"][:, 0, n:n + 1], base[:, n, :], ALU.mult, ALU.add))
            link.settle()
            for n in range(TILES):
                added(v.scalar_tensor_tensor(m["R"][:, n, :], m["G"][1][:, n, :], m["w"][:, 1, n:n + 1], m["R"][:, n, :], ALU.mult, ALU.add))
            dve.wait_ge(added.sem, TILES)

        if layer == 1:
            @block.scalar
            def _(act):
                for k in range(2):
                    act.wait_ge(stats.sem, k + 1)
                    rooted(nc.scalar.activation(m["root"][:, :], m["std"][:, :], ACT.Sqrt))


INNER = 256
NH, HP = 4, 64
NS = 64
NANG = NS // 2
Z0, X0, B0, DT0, DA0, TR0, AN0, PROJ = 0, 256, 512, 640, 644, 648, 652, 684
TWO_PI = 2.0 * math.pi
PI_PARTS = [6.28125, 0.0019350051879882812, 3.019915e-07]


def stage_ssm_project(nc, m, ctx, A):
    def sg(name):
        return Signal(ctx, nc, "sp_" + name)

    x_ps, x_sb, a_ps, b_ps, a_sb, b_sb = sg("x_ps"), sg("x_sb"), sg("a_ps"), sg("b_ps"), sg("a_sb"), sg("b_sb")
    first = ctx.new("ssm_loads")
    m["load1"] = ctx.new("layer1_loads")
    bank = m["bank"]
    with nc.Block() as block:
        @block.sync
        def _(sp):
            sp.dma_start(m["Win"][:, :], A["L1_attn_W_in"]).then_inc(first, 16)
            sp.dma_start(m["Wout"][:, :, :], A["L1_attn_W_out"].rearrange("(c p) d -> p c d", p=P)).then_inc(first, 16)

            def row(dst, src):
                sp.dma_start(dst, src.rearrange("(o n) -> o n", o=1).to_broadcast([P, src.shape[0]])).then_inc(first, 16)

            row(m["dtb"][:, :], A["L1_attn_dt_bias"])
            row(m["Dp"][:, :], A["L1_attn_D_param"])
            row(m["lng"][:, 0, :], A["L1_attn_Bn_g"])
            row(m["lng"][:, 1, :], A["L1_attn_Cn_g"])
            row(m["lnb"][:, 0, :], A["L1_attn_Bn_b"])
            row(m["lnb"][:, 1, :], A["L1_attn_Cn_b"])
            for dst, src in ((m["Wr1"][:, :], A["L1_ffn_router_w"]),
                             (m["w1"][:, :, :], A["L1_ffn_w1"].rearrange("e p h -> p e h")),
                             (m["w2"][:, :, :], A["L1_ffn_w2"].rearrange("e (c p) d -> p (e c) d", p=P))):
                sp.dma_start(dst, src).then_inc(m["load1"], 16)
            m["load1_n"] = 16 * 3
            sp.wait_ge(first, 16 * 8)

        @block.tensor
        def _(pe):
            transpose_x(nc, pe, m, x_ps, x_sb, (0, 1))
            pe.wait_ge(first, 16 * 8)
            for n in range(TILES):
                pe.wait_ge(x_sb.sem, n // 4 + 1)
                if n >= 2:
                    pe.wait_ge(a_sb.sem, n - 1)
                    pe.wait_ge(b_sb.sem, n - 1)
                xT = m["XT"][:, n * P:(n + 1) * P]
                a_ps(nc.tensor.matmul(bank(2 + n % 2), lhsT=xT, rhs=m["Win"][:, 0:512], start=True, stop=True))
                b_ps(nc.tensor.matmul(bank(4 + n % 2)[:, 0:PROJ - 512], lhsT=xT, rhs=m["Win"][:, 512:PROJ], start=True, stop=True))

        @block.scalar
        def _(act):
            copy_xt(nc, act, m, x_ps, x_sb, (0, 1))
            for n in range(TILES):
                act.wait_ge(a_ps.sem, n + 1)
                a_sb(nc.scalar.copy(m["PJ"][:, n, 0:512], bank(2 + n % 2)))

        @block.vector
        def _(dve):
            for n in range(TILES):
                dve.wait_ge(b_ps.sem, n + 1)
                b_sb(nc.vector.tensor_copy(m["PJ"][:, n, 512:PROJ], bank(4 + n % 2)[:, 0:PROJ - 512]))
            dve.wait_ge(b_sb.sem, TILES)


def stage_ssm_gates(nc, m, ctx):
    def sg(name):
        return Signal(ctx, nc, "sg_" + name)

    to_act, from_act, to_pe, from_pe, rows = sg("to_act"), sg("from_act"), sg("to_pe"), sg("from_pe"), sg("rows")
    shifted = ctx.new("sg_shifted")
    bank = m["bank"]
    PJ = m["PJ"]
    x4 = PJ[:, :, X0:B0]
    with nc.Block() as block:
        @block.vector
        def _(dve):
            v = nc.vector
            link = Chain(ctx, nc, dve, "sg_chain")
            acts = [0]

            def act_turn(ins):
                to_act(ins)
                acts[0] += 1
                return acts[0]

            link(v.tensor_tensor(m["sp"][:, :, 0:NH], PJ[:, :, DT0:DA0], bcast_mid(m["dtb"][:, :], TILES), ALU.add))
            link(v.tensor_copy(m["sp"][:, :, NH:2 * NH], PJ[:, :, DA0:TR0]))
            link(v.tensor_scalar(m["sq"][:, :, :], m["sp"][:, :, :], -1.0, None, ALU.mult))
            act_turn(v.tensor_tensor(m["sq"][:, :, :], m["sq"][:, :, :], m["sp"][:, :, :], ALU.max))
            BCp = PJ[:, :, B0:DT0].rearrange("p t (k n) -> p t k n", k=2)

            def stat(ap):
                return ap[:, :, :].unsqueeze(3).to_broadcast([P, TILES, 2, NS])

            def gb(ap):
                return ap[:, :, :].unsqueeze(1).to_broadcast([P, TILES, 2, NS])

            link(v.tensor_reduce(m["mean"][:, :, :], BCp, AX, ALU.add))
            link(v.tensor_scalar(m["mean"][:, :, :], m["mean"][:, :, :], 1.0 / NS, None, ALU.mult))
            link(v.tensor_tensor(m["BC"][:, :, :, :], BCp, stat(m["mean"]), ALU.subtract))
            link(v.tensor_tensor(m["BCt"][:, :, :, :], m["BC"][:, :, :, :], m["BC"][:, :, :, :], ALU.mult))
            link(v.tensor_reduce(m["var"][:, :, :], m["BCt"][:, :, :, :], AX, ALU.add))
            dve.wait_ge(from_act.sem, 1)
            link(v.tensor_scalar(m["sq"][:, :, :], m["sq"][:, :, :], 1.0, None, ALU.add))
            act_turn(v.tensor_scalar(m["sp"][:, :, :], m["sp"][:, :, :], 0.0, None, ALU.max))
            dve.wait_ge(from_act.sem, 3)
            link(v.tensor_scalar(m["te"][:, :, :], m["te"][:, :, :], 1.0, None, ALU.add))
            link(v.reciprocal(m["te"][:, :, :], m["te"][:, :, :]))
            dve.wait_ge(from_act.sem, 4)
            link(v.tensor_scalar(m["sz"][:, :, :], m["sz"][:, :, :], 1.0, None, ALU.add))
            link(v.reciprocal(m["sz"][:, :, :], m["sz"][:, :, :]))
            link(v.tensor_tensor(m["sz"][:, :, :], m["sz"][:, :, :], PJ[:, :, Z0:X0], ALU.mult))
            link(v.tensor_tensor(m["sp"][:, :, :], m["sp"][:, :, :], m["sq"][:, :, :], ALU.add))
            DT = m["sp"][:, :, 0:NH]
            link(v.tensor_scalar(m["adt"][:, :, :], m["sp"][:, :, NH:2 * NH], -1.0, -1e-4, ALU.mult, ALU.min))
            link(v.tensor_tensor(m["adt"][:, :, :], m["adt"][:, :, :], DT, ALU.mult))
            link(v.tensor_tensor(m["ca"][:, :, :], DT, m["te"][:, :, :], ALU.mult))
            link(v.tensor_tensor(m["cb"][:, :, :], DT, m["ca"][:, :, :], ALU.subtract))
            link(v.tensor_tensor(m["cb"][:, :, :], m["cb"][:, :, :], bcast_last(m["inner"][:, :], NH), ALU.mult))
            link(v.tensor_reduce(m["dtm"][:, :], DT, AX, ALU.add))
            link(v.tensor_scalar(m["dtm"][:, :], m["dtm"][:, :], 1.0 / NH, None, ALU.mult))
            to_pe(v.tensor_tensor(m["av"][:, :, :], PJ[:, :, AN0:PROJ], bcast_last(m["dtm"][:, :], NANG), ALU.mult))
            act_turn(v.tensor_scalar(m["var"][:, :, :], m["var"][:, :, :], 1.0 / NS, 1e-5, ALU.mult, ALU.add))
            dve.wait_ge(from_pe.sem, 1)
            link(v.tensor_copy(m["Lc"][:, :, :], bank(1)[:, 0:TILES * NH].rearrange("p (t h) -> p t h", h=NH)))
            link(v.tensor_copy(m["Le"][:, :, :], bank(2)[:, 0:TILES * NH].rearrange("p (t h) -> p t h", h=NH)))
            act_turn(v.tensor_tensor(m["Ld"][:, :, :], m["Le"][:, :, :], m["Lc"][:, :, :], ALU.subtract))
            for k in range(2):
                r, t = m["ang"][:, k, :], m["turns"][:, :]
                link(v.tensor_copy(r, bank(0)))
                link(v.tensor_scalar(t, r, 1.0 / TWO_PI, 0.25 * k, ALU.mult, ALU.add))
                link(v.tensor_scalar(t, t, ROUND_MAGIC, None, ALU.add))
                link(v.tensor_scalar(t, t, ROUND_MAGIC, None, ALU.subtract))
                for c in PI_PARTS:
                    link(v.scalar_tensor_tensor(r, t, -c, r, ALU.mult, ALU.add))
                if k == 1:
                    link(v.tensor_scalar(r, r, math.pi / 2, None, ALU.add))
                act_turn(v.tensor_scalar(r, r, 3.1415925, -3.1415925, ALU.min, ALU.max))
            dve.wait_ge(from_act.sem, 5)
            link(v.reciprocal(m["var"][:, :, :], m["var"][:, :, :]))
            link(v.tensor_tensor(m["BC"][:, :, :, :], m["BC"][:, :, :, :], stat(m["var"]), ALU.mult))
            link(v.tensor_tensor(m["BC"][:, :, :, :], m["BC"][:, :, :, :], gb(m["lng"]), ALU.mult))
            link(v.tensor_tensor(m["BC"][:, :, :, :], m["BC"][:, :, :, :], gb(m["lnb"]), ALU.add))
            dve.wait_ge(from_act.sem, 10)
            for k in range(2):
                pair = m["BC"][:, :, k, :].rearrange("p t (n two) -> p t n two", two=2)
                dst = m["BCt"][:, :, k, :].rearrange("p t (n two) -> p t n two", two=2)
                sin, cos = (m["ang"][:, i, :].rearrange("p (t n) -> p t n", n=NANG) for i in range(2))
                tmp = m["turns"][:, :].rearrange("p (t n) -> p t n", n=NANG)
                ev, od = pair[:, :, :, 0], pair[:, :, :, 1]
                link(v.tensor_tensor(dst[:, :, :, 0], ev, cos, ALU.mult))
                link(v.tensor_tensor(tmp, od, sin, ALU.mult))
                link(v.tensor_tensor(dst[:, :, :, 0], dst[:, :, :, 0], tmp, ALU.subtract))
                link(v.tensor_tensor(dst[:, :, :, 1], ev, sin, ALU.mult))
                link(v.tensor_tensor(tmp, od, cos, ALU.mult))
                if k == 0:
                    rows(v.tensor_tensor(dst[:, :, :, 1], dst[:, :, :, 1], tmp, ALU.add))
                else:
                    link(v.tensor_tensor(dst[:, :, :, 1], dst[:, :, :, 1], tmp, ALU.add))
                dve.wait_ge(rows.sem, 1)

        @block.scalar
        def _(act):
            s = nc.scalar
            act.wait_ge(to_act.sem, 1)
            from_act(s.activation(m["sq"][:, :, :], m["sq"][:, :, :], ACT.Exp, scale=-1.0))
            act.wait_ge(to_act.sem, 2)
            from_act(s.activation(m["sq"][:, :, :], m["sq"][:, :, :], ACT.Ln))
            from_act(s.activation(m["te"][:, :, :], PJ[:, :, TR0:AN0], ACT.Exp, scale=-1.0))
            from_act(s.activation(m["sz"][:, :, :], PJ[:, :, Z0:X0], ACT.Exp, scale=-1.0))
            act.wait_ge(to_act.sem, 3)
            from_act(s.activation(m["var"][:, :, :], m["var"][:, :, :], ACT.Sqrt))
            act.wait_ge(to_act.sem, 4)
            from_act(s.activation(m["eL"][:, :, :], m["Lc"][:, :, :], ACT.Exp))
            from_act(s.activation(m["eE"][:, :, :], m["Le"][:, :, :], ACT.Exp))
            from_act(s.activation(m["eD"][:, :, :], m["Ld"][:, :, :], ACT.Exp))
            for k in range(2):
                act.wait_ge(to_act.sem, 5 + k)
                from_act(s.activation(m["ang"][:, k, :], m["ang"][:, k, :], ACT.Sin))

        @block.tensor
        def _(pe):
            pe.wait_ge(to_pe.sem, 1)
            adt = m["adt"][:, :, :].rearrange("p t h -> p (t h)")
            nc.tensor.matmul(bank(1)[:, 0:TILES * NH], lhsT=m["tri"][:, :], rhs=adt, start=True, stop=True)
            nc.tensor.matmul(bank(2)[:, 0:TILES * NH], lhsT=m["ones"][:, :], rhs=adt, start=True, stop=True)
            for n in range(TILES):
                out = bank(0)[:, n * NANG:(n + 1) * NANG]
                before = range(n // TPB * TPB, n)
                last = nc.tensor.matmul(out, lhsT=m["tri"][:, :], rhs=m["av"][:, n, :], start=True, stop=not before)
                for c in before:
                    last = nc.tensor.matmul(out, lhsT=m["ones"][:, :], rhs=m["av"][:, c, :], start=False, stop=c == n - 1)
            from_pe(last)

        @block.sync
        def _(sp):
            def shift(dst, src):
                sp.dma_start(dst[1:P, :, :], src[0:P - 1, :, :]).then_inc(shifted, 16)
                sp.dma_start(dst[0:1, 1:TILES, :], src[P - 1:P, 0:TILES - 1, :]).then_inc(shifted, 16)
                sp.dma_start(dst[0:1, 0:1, :], m["zeros"][0:1, 0:dst.shape[2]].unsqueeze(1)).then_inc(shifted, 16)

            shift(m["xsh"][:, :, :], x4)
            sp.wait_ge(rows.sem, 1)
            shift(m["Bsh"][:, :, :], m["BCt"][:, :, 0, :])
            sp.wait_ge(shifted, 16 * 6)


def stage_ssm_scan(nc, m, ctx):
    def sg(name):
        return Signal(ctx, nc, "ss_" + name)

    t_ps, t_sb, g_ps, l_in, l_ps, e_in, e_sb = (sg(x) for x in ("t_ps", "t_sb", "g_ps", "l_in", "l_ps", "e_in", "e_sb"))
    wgt, xab, xe, y_ps, i_ps, st_ps, st_sb, y_sb = (sg(x) for x in ("wgt", "xab", "xe", "y_ps", "i_ps", "st_ps", "st_sb", "y_sb"))
    yT_ps, yT_sb, o_ps, r_sb = (sg(x) for x in ("yT_ps", "yT_sb", "o_ps", "r_sb"))
    bank = m["bank"]

    def h4(ap, n):
        return ap.rearrange("p (h x) -> p h x", h=NH) if n else ap

    with nc.Block() as block:
        @block.tensor
        def _(pe):
            def front(n):
                if n >= 1:
                    pe.wait_ge(t_sb.sem, n)
                for i, src in enumerate((m["BCt"][:, n, 0, :], m["Bsh"][:, n, :], m["BCt"][:, n, 1, :])):
                    last = nc.tensor.transpose(bank(0)[0:NS, i * P:(i + 1) * P], src, m["ident"][:, :])
                t_ps(last)
                pe.wait_ge(l_in.sem, n + 1)
                if n >= 2:
                    pe.wait_ge(e_in.sem, n - 1)
                nc.tensor.matmul(bank(2 + n % 2), lhsT=m["ones"][:, :], rhs=m["adtri"][:, n % 2, :, :].rearrange("p h t -> p (h t)"),
                                 start=True, stop=False)
                l_ps(nc.tensor.matmul(bank(2 + n % 2), lhsT=m["identb"][:, :], rhs=m["causal"][:, :, :].rearrange("p h t -> p (h t)"),
                                      start=False, stop=True))
                pe.wait_ge(t_sb.sem, n + 1)
                if n >= 1:
                    pe.wait_ge(wgt.sem, 2 * n)
                for i in range(2):
                    last = nc.tensor.matmul(bank(1)[:, i * P:(i + 1) * P], lhsT=m["BT"][:, n % 2, i, :], rhs=m["BT"][:, n % 2, 2, :],
                                            start=True, stop=True)
                g_ps(last)

            def back(n):
                pe.wait_ge(xe.sem, n + 1)
                if n >= 1:
                    pe.wait_ge(st_sb.sem, n)
                out = bank(6)[0:NS, 0:INNER]
                nc.tensor.matmul(out, lhsT=m["BCt"][:, n, 0, :], rhs=m["xae"][:, n % 2, 0, :], start=True, stop=False)
                st_ps(nc.tensor.matmul(out, lhsT=m["Bsh"][:, n, :], rhs=m["xae"][:, n % 2, 1, :], start=False, stop=True))
                if n >= 2:
                    pe.wait_ge(y_sb.sem, n - 1)
                yb = bank(4 + n % 2)
                if n % TPB:
                    i_ps(nc.tensor.matmul(yb[:, INNER:2 * INNER], lhsT=m["BT"][:, n % 2, 2, :], rhs=m["H"][:, n % 2, :],
                                          start=True, stop=True))
                pe.wait_ge(wgt.sem, 2 * (n + 1))
                for h in range(NH):
                    for i in range(2):
                        last = nc.tensor.matmul(yb[:, h * HP:(h + 1) * HP], lhsT=m["W"][:, n % 2, i, h, :],
                                                rhs=m["xab"][:, n % 2, i, h * HP:(h + 1) * HP], start=i == 0, stop=i == 1)
                y_ps(last)

            def project(n):
                pe.wait_ge(y_sb.sem, n + 1)
                if n >= 1:
                    pe.wait_ge(r_sb.sem, n)
                for k in range(2):
                    last = nc.tensor.transpose(bank(7)[:, k * P:(k + 1) * P], m["yg"][:, n % 2, k * P:(k + 1) * P], m["ident"][:, :])
                yT_ps(last)
                pe.wait_ge(yT_sb.sem, n + 1)
                for k in range(2):
                    last = nc.tensor.matmul(bank(7)[:, 2 * P:3 * P], lhsT=m["yT"][:, k * P:(k + 1) * P], rhs=m["Wout"][:, k, :],
                                            start=k == 0, stop=k == 1)
                o_ps(last)

            front(0)
            for n in range(TILES):
                if n + 1 < TILES:
                    front(n + 1)
                back(n)
                if n >= 1:
                    project(n - 1)
            project(TILES - 1)

        @block.vector
        def _(dve):
            v = nc.vector
            link = Chain(ctx, nc, dve, "ss_chain")

            def rows(n):
                if n >= 2:
                    dve.wait_ge(l_ps.sem, n - 1)
                l_in(v.tensor_tensor(m["adtri"][:, n % 2, :, :], bcast_mid(m["tri"][:, :], NH), bcast_last(m["adt"][:, n, :], P), ALU.mult))

            def exponents(n):
                dve.wait_ge(l_ps.sem, n + 1)
                if n >= 2:
                    dve.wait_ge(wgt.sem, 2 * (n - 1))
                e_in(v.tensor_tensor(m["Ex"][:, n % 2, :, :], bank(2 + n % 2).rearrange("p (h t) -> p h t", h=NH),
                                     bcast_last(m["Lc"][:, n, :], P), ALU.subtract))

            def inputs(n):
                if n >= 2:
                    dve.wait_ge(y_ps.sem, n - 1)
                for i, (src, coef) in enumerate(((m["PJ"][:, n, X0:B0], m["ca"]), (m["xsh"][:, n, :], m["cb"]))):
                    link(v.tensor_tensor(h4(m["xab"][:, n % 2, i, :], 1), h4(src, 1), bcast_last(coef[:, n, :], HP), ALU.mult))
                    ins = v.tensor_tensor(h4(m["xae"][:, n % 2, i, :], 1), h4(m["xab"][:, n % 2, i, :], 1),
                                          bcast_last(m["eD"][:, n, :], HP), ALU.mult)
                    if i == 0:
                        link(ins)
                    else:
                        xe(ins)

            def weights(n):
                dve.wait_ge(g_ps.sem, n + 1)
                dve.wait_ge(e_sb.sem, n + 1)
                if n >= 2:
                    dve.wait_ge(y_ps.sem, n - 1)
                for i in range(2):
                    wgt(v.tensor_tensor(m["W"][:, n % 2, i, :, :], m["Ex"][:, n % 2, :, :], bcast_mid(bank(1)[:, i * P:(i + 1) * P], NH),
                                        ALU.mult))

            def state(n):
                dve.wait_ge(st_ps.sem, n + 1)
                src = bank(6)[0:NS, 0:INNER]
                dst = m["H"][:, (n + 1) % 2, :]
                if n % TPB == 0:
                    st_sb(v.tensor_copy(dst, src))
                else:
                    if n >= 2:
                        dve.wait_ge(i_ps.sem, (n - 1) - (n - 1) // TPB)
                    link(v.tensor_tensor(h4(dst, 1), h4(m["H"][:, n % 2, :], 1), bcast_last(m["eE"][0:NS, n, :], HP), ALU.mult))
                    st_sb(v.tensor_tensor(dst, dst, src, ALU.add))
                dve.wait_ge(st_sb.sem, n + 1)

            def output(n):
                dve.wait_ge(y_ps.sem, n + 1)
                yb = bank(4 + n % 2)
                if n >= 2:
                    dve.wait_ge(yT_ps.sem, n - 1)
                y = m["yg"][:, n % 2, :]
                link(v.tensor_tensor(h4(y, 1), h4(m["PJ"][:, n, X0:B0], 1), bcast_last(m["Dp"][:, :], HP), ALU.mult))
                link(v.tensor_tensor(y, y, yb[:, 0:INNER], ALU.add))
                if n % TPB:
                    link(v.tensor_tensor(h4(m["inter"][:, :], 1), h4(yb[:, INNER:2 * INNER], 1), bcast_last(m["eL"][:, n, :], HP), ALU.mult))
                    link(v.tensor_tensor(y, y, m["inter"][:, :], ALU.add))
                y_sb(v.tensor_tensor(y, y, m["sz"][:, n, :], ALU.mult))

            def residual(n):
                dve.wait_ge(o_ps.sem, n + 1)
                r_sb(v.tensor_tensor(m["R"][:, n, :], bank(7)[:, 2 * P:3 * P], m["X"][:, n, :], ALU.add))

            rows(0)
            exponents(0)
            inputs(0)
            for n in range(TILES):
                if n + 1 < TILES:
                    rows(n + 1)
                weights(n)
                state(n)
                if n + 1 < TILES:
                    exponents(n + 1)
                    inputs(n + 1)
                output(n)
                if n >= 1:
                    residual(n - 1)
            residual(TILES - 1)
            dve.wait_ge(r_sb.sem, TILES)

        @block.scalar
        def _(act):
            def copies(n):
                act.wait_ge(t_ps.sem, n + 1)
                if n >= 2:
                    act.wait_ge(y_ps.sem, n - 1)
                    if (n - 2) % TPB:
                        act.wait_ge(i_ps.sem, (n - 2) - (n - 2) // TPB)
                t_sb(nc.scalar.copy(m["BT"][:, n % 2, :, :], bank(0)[0:NS, 0:3 * P].rearrange("p (k t) -> p k t", k=3)))

            def decays(n):
                act.wait_ge(e_in.sem, n + 1)
                e_sb(nc.scalar.activation(m["Ex"][:, n % 2, :, :], m["Ex"][:, n % 2, :, :], ACT.Exp))

            def yT(n):
                act.wait_ge(yT_ps.sem, n + 1)
                if n >= 1:
                    act.wait_ge(o_ps.sem, n)
                yT_sb(nc.scalar.copy(m["yT"][:, :], bank(7)[:, 0:2 * P]))

            copies(0)
            decays(0)
            for n in range(TILES):
                if n + 1 < TILES:
                    copies(n + 1)
                    decays(n + 1)
                if n >= 1:
                    yT(n - 1)
            yT(TILES - 1)


def build(nc, A, out, stop=99):
    NT0, NT1 = 44, 40
    m = {}
    top = ExitStack()
    with top:
        made = {}

        def alloc(scope, **shapes):
            for name, (shape, dt) in shapes.items():
                made[name] = made.get(name, 0) + 1
                m[name] = scope.enter_context(nc.sbuf_tensor(f"{name}_{made[name]}", shape, dt))

        sems = Semaphores(nc)
        m["PS"] = top.enter_context(nc.psum_tensor("banks", [P, 8 * 512], FP32))
        m["bank"] = lambda i: m["PS"][:, i * 512:(i + 1) * 512]
        alloc(top, ident=([P, P], FP32), identb=([P, P], BF16), tri=([P, P], FP32), tri_strict=([P, P], FP32),
              ones=([P, P], FP32), ones3=([3, P], BF16), band=([P, 2, 256], BF16), causal=([P, 4, P], BF16),
              zeros=([P, 256], FP32), inner=([P, TILES], FP32), iota_e=([P, TILES, 12], FP32), iota_j=([P, NT0], FP32),
              X=([P, TILES, D], FP32), R=([P, TILES, D], FP32),
              bn=([P, TILES, 6], FP32), mv=([P, TILES, 2], FP32), std=([P, TILES], FP32), root=([P, TILES], FP32),
              rstd=([P, TILES], FP32), flag=([1, 4], BF16),
              top=([P, 2, TILES], FP32), first=([P, TILES], FP32), gap=([P, TILES], FP32), gexp=([P, TILES], FP32),
              cnt=([P, 12], FP32), start=([P, 12], FP32), base=([P, 12], FP32), posf=([P, 2, TILES], FP32),
              pos=([P, 2, TILES], I32), choice=([P, 2, TILES], I32), w=([P, 2, TILES], FP32),
              eidf=([1, NT0], FP32), eid=([1, NT0], I32))
        m["xs"] = [nc.dram_tensor(f"slots_in{l}", [nt * P, D], FP32, kind="Internal").ap() for l, nt in enumerate((NT0, NT1))]
        m["ys"] = [nc.dram_tensor(f"slots_out{l}", [nt * P, D], FP32, kind="Internal").ap() for l, nt in enumerate((NT0, NT1))]
        m["qk_dram"] = nc.dram_tensor("qk_parts", [2, BATCH, 3, P, SEQ], BF16, kind="Internal").ap()
        m["gamma_dram"], m["beta_dram"] = A["L1_ffn_gamma"], A["L1_ffn_beta"]
        m["bias3"] = [None, None]

        def biases(scope, l, E, W, b_up, b_down):
            m["bias3"][l] = scope.enter_context(nc.sbuf_tensor(f"bias3_{l}", [3, E * W], BF16))
            with ExitStack() as tmp:
                m["be"] = tmp.enter_context(nc.sbuf_tensor(f"bias_rest{l}", [E, W], FP32))
                m["be_parts"] = tmp.enter_context(nc.sbuf_tensor(f"bias_parts{l}", [E, 3, W], BF16))
                stage_bias(nc, m, sems, l, b_up, b_down)

        make_constants(nc, m, sems)

        layer0 = ExitStack()
        with layer0:
            alloc(layer0, br=([P, 12], FP32), bs2=([P, D], FP32), Wr0=([P, 12], FP32), Ws1=([P, 512], FP32),
                  Ws2=([P, 2, D], FP32), bs1=([P, 4], FP32), We1=([P, 12, 768], FP32), We2=([P, 36, D], FP32))
            biases(layer0, 0, 12, 896, A["L0_ffn_be1"], A["L0_ffn_be2"])
            with ExitStack() as att:
                alloc(att, WT=([P, 4 * D], FP32), bv=([P, D], FP32), bo=([P, D], FP32), Vext=([P, 20, HEADS, HD + 1], FP32),
                      qrep=([P, 2, 8, SEQ], BF16), krep=([P, 2, 8, SEQ], BF16))
                with ExitStack() as proj:
                    alloc(proj, Wraw=([P, 4 * D], FP32), bqk=([P, 2], FP32), q3=([P, 3, SEQ], BF16), k3=([P, 3, SEQ], BF16),
                          rest=([P, SEQ], FP32), XT=([P, TOK], FP32))
                    stage_load(nc, m, sems, A)
                    stage_project(nc, m, sems)
                alloc(att, PT=([P, 3, HEADS, 256], FP32), mx=([P, TILES * HEADS], FP32), m3=([HEADS, 3, SEQ], BF16),
                      mrest=([HEADS, P], FP32), rden=([P, HEADS], FP32), ctx=([P, 2, D], FP32), ctxT=([P, D], FP32))
                stage_attention(nc, m, sems)
            stage_layernorm(nc, m, sems, "ln0", out if stop == 0 else None)
            if stop == 0:
                return
            def tiles(scope):
                alloc(scope, XT=([P, TOK], FP32), xin=([P, 2, D], FP32), xTt=([P, 2, P], FP32), gate=([P, 2, 512], FP32), act_sb=([P, 2, 512], FP32),
                      actT=([P, 2, 512], FP32), y_sb=([P, 2, D], FP32))
                alloc(scope, cmp=([1, NT0 * 12], FP32))
                l = made["cmp"] - 1
                m["rt"] = [scope.enter_context(nc.sbuf_tensor(f"route{l}_tmp{i}", [P, TILES * 12], FP32)) for i in range(6)]
                m["G"] = [scope.enter_context(nc.sbuf_tensor(f"gathered{l}_{k}", [P, TILES, D], FP32)) for k in range(2)]

            with ExitStack() as moe:
                tiles(moe)
                alloc(moe, sh_gate=([P, 2, 512], FP32), sh_act=([P, 2, 512], FP32))
                stage_router(nc, m, sems, 0, 12, 1.5, NT0, m["Wr0"], m["br"], True)
                stage_experts(nc, m, sems, 0, NT0, 384, m["We1"], m["We2"], m["bias3"][0], 12)
                stage_combine(nc, m, sems, 0)
        stage_layernorm(nc, m, sems, "ln1", out if stop == 1 else None)
        if stop == 1:
            return
        sems.close()
        sems = Semaphores(nc)
        with ExitStack() as layer1:
            alloc(layer1, Wr1=([P, 8], FP32), w1=([P, 8, 512], FP32), w2=([P, 32, D], FP32))
            biases(layer1, 1, 8, 640, A["L1_ffn_b1"], A["L1_ffn_b2"])
            with ExitStack() as ssm:
                alloc(ssm, Win=([P, PROJ], FP32), Wout=([P, 2, D], FP32), dtb=([P, NH], FP32), Dp=([P, NH], FP32),
                      lng=([P, 2, NS], FP32), lnb=([P, 2, NS], FP32), PJ=([P, TILES, PROJ], FP32), sz=([P, TILES, INNER], FP32),
                      adt=([P, TILES, NH], FP32), ca=([P, TILES, NH], FP32), cb=([P, TILES, NH], FP32), te=([P, TILES, NH], FP32),
                      Lc=([P, TILES, NH], FP32), Le=([P, TILES, NH], FP32), Ld=([P, TILES, NH], FP32),
                      eL=([P, TILES, NH], FP32), eE=([P, TILES, NH], FP32), eD=([P, TILES, NH], FP32),
                      BCt=([P, TILES, 2, NS], FP32), xsh=([P, TILES, INNER], FP32), Bsh=([P, TILES, NS], FP32))
                with ExitStack() as proj:
                    alloc(proj, XT=([P, TOK], FP32))
                    stage_ssm_project(nc, m, sems, A)
                with ExitStack() as gates:
                    alloc(gates, sp=([P, TILES, 8], FP32), sq=([P, TILES, 8], FP32), mean=([P, TILES, 2], FP32),
                          var=([P, TILES, 2], FP32), BC=([P, TILES, 2, NS], FP32), dtm=([P, TILES], FP32),
                          av=([P, TILES, NANG], FP32), ang=([P, 2, TILES * NANG], FP32), turns=([P, TILES * NANG], FP32))
                    stage_ssm_gates(nc, m, sems)
                with ExitStack() as scan:
                    alloc(scan, adtri=([P, 2, NH, P], FP32), Ex=([P, 2, NH, P], FP32), W=([P, 2, 2, NH, P], FP32),
                          BT=([NS, 2, 3, P], FP32), xab=([P, 2, 2, INNER], FP32), xae=([P, 2, 2, INNER], FP32),
                          H=([NS, 2, INNER], FP32), yg=([P, 2, INNER], FP32), inter=([P, INNER], FP32), yT=([P, INNER], FP32))
                    stage_ssm_scan(nc, m, sems)
            stage_layernorm(nc, m, sems, "ln2", out if stop == 2 else None)
            if stop == 2:
                return
            with ExitStack() as moe:
                tiles(moe)
                m["Gam"] = [moe.enter_context(nc.sbuf_tensor(f"gamma_rows{k}", [P, TILES, D], FP32)) for k in range(2)]
                m["Bet"] = [moe.enter_context(nc.sbuf_tensor(f"beta_rows{k}", [P, TILES, D], FP32)) for k in range(2)]
                stage_router(nc, m, sems, 1, 8, 1.0, NT1, m["Wr1"], None, False)
                stage_experts(nc, m, sems, 1, NT1, 512, m["w1"], m["w2"], m["bias3"][1], 8)
                stage_combine(nc, m, sems, 1)
            stage_layernorm(nc, m, sems, "ln3", out)


def kernel(**inputs):
    import numpy as _np
    import concourse.bacc as _bacc
    from concourse import mybir as _mybir
    from concourse.bass_utils import run_bass_kernel_spmd as _run

    nc = _bacc.Bacc("TRN2", target_bir_lowering=False, num_devices=1)
    arrays, args = {}, {}
    for name in inputs:
        a = _np.ascontiguousarray(inputs[name])
        arrays[f"in_{name}"] = a
        args[name] = nc.dram_tensor(f"in_{name}", a.shape, _mybir.dt.from_np(a.dtype), kind="ExternalInput").ap()
    out = nc.dram_tensor("out_dram", (BATCH, SEQ, D), _mybir.dt.float32, kind="ExternalOutput").ap()
    build(nc, args, out)
    r = _run(nc, [arrays], core_ids=[0])
    return r.results[0]["out_dram"]
```

```python
import concourse.bass as bass
from concourse import mybir
from contextlib import ExitStack
import math

FP32 = mybir.dt.float32
BF16 = mybir.dt.bfloat16
I32 = mybir.dt.int32
ALU = mybir.AluOpType
ACT = mybir.ActivationFunctionType
AX = mybir.AxisListType.X

P = 128
D = 128
BATCH, SEQ = 4, 512
TOK = BATCH * SEQ
TILES = TOK // P
TPB = SEQ // P
HEADS, HD = 16, 8
HALF = 64
MASKED = -1.0e30
Q_PARTS = [0, 0, 0, 1, 1, 2]
K_PARTS = [0, 1, 2, 0, 1, 0]
QK_ROWS = HD * len(Q_PARTS)
MAX_PARTS = 3
ROUND_MAGIC = 12582912.0


class Semaphores:

    def __init__(self, nc):
        self.nc, self.all = nc, []

    def new(self, name):
        self.all.append(self.nc.alloc_semaphore(name=name))
        return self.all[-1]

    def close(self):
        self.nc.clear_and_free_semaphores(self.all)
        self.nc.all_engine_barrier()


class Signal:

    def __init__(self, ctx, nc, name):
        self.sem = ctx.new(name)
        self.n = 0

    def __call__(self, ins):
        ins.then_inc(self.sem, 1)
        self.n += 1
        return self.n


class Chain:

    def __init__(self, ctx, nc, eng, name):
        self.eng, self.sem, self.n = eng, ctx.new(name), 0

    def __call__(self, ins):
        ins.then_inc(self.sem, 1)
        self.n += 1
        self.eng.wait_ge(self.sem, self.n)

    def loose(self, ins):
        ins.then_inc(self.sem, 1)
        self.n += 1

    def settle(self):
        self.eng.wait_ge(self.sem, self.n)


def bcast_mid(ap, n):
    return ap.unsqueeze(1).to_broadcast([ap.shape[0], n, ap.shape[1]])


def bcast_last(ap, n):
    return ap.unsqueeze(2).to_broadcast([ap.shape[0], ap.shape[1], n])


def stage_begin(nc, m, ctx, A):
    done = Signal(ctx, nc, "constants_done")
    filled = Signal(ctx, nc, "constants_filled")
    sem = ctx.new("loads")
    ones = Signal(ctx, nc, "ones_columns")
    bias = bias_signals(nc, ctx, 0)
    with nc.Block() as block:
        @block.gpsimd
        def _(pool):
            g = nc.gpsimd
            for t, v in ((m["ident"], 0.0), (m["identb"], 0.0), (m["tri"], 1.0), (m["tri_strict"], 1.0), (m["ones"], 1.0)):
                filled(g.memset(t[:, :], v))
            filled(g.memset(m["band"][:, :, :], 0.0))
            filled(g.memset(m["causal"][:, :, :], 0.0))
            filled(g.memset(m["ones3"][:, :], 1.0))
            filled(g.memset(m["zeros"][:, :], 0.0))
            filled(g.memset(m["inner"][:, :], 1.0))
            filled(g.iota(m["iota_e"][:, :, :], pattern=[[0, TILES], [1, 12]], base=0, channel_multiplier=0,
                          allow_small_or_imprecise_dtypes=True))
            filled(g.iota(m["iota_p"][:, :], pattern=[[0, 1]], base=0, channel_multiplier=1,
                          allow_small_or_imprecise_dtypes=True))
            filled(g.iota(m["iota_slot"][:, :], pattern=[[P, m["iota_slot"].shape[1]]], base=2 * TOK, channel_multiplier=1,
                          allow_small_or_imprecise_dtypes=True))
            filled(g.iota(m["iota_j"][:, :], pattern=[[1, m["iota_j"].shape[1]]], base=0, channel_multiplier=0,
                          allow_small_or_imprecise_dtypes=True))
            pool.wait_ge(filled.sem, filled.n)

            def select(t, pattern, base, mult, fill, op=ALU.is_ge):
                done(g.affine_select(out=t, in_=t, compare_op=op, fill=fill, base=base, pattern=pattern,
                                     channel_multiplier=mult))
                pool.wait_ge(done.sem, done.n)

            select(m["ident"][:, :], [[-1, P]], 0, 1, 1.0, ALU.not_equal)
            select(m["identb"][:, :], [[-1, P]], 0, 1, 1.0, ALU.not_equal)
            select(m["tri"][:, :], [[1, P]], 0, -1, 0.0)
            select(m["tri_strict"][:, :], [[1, P]], -1, -1, 0.0)
            select(m["band"][:, :, :], [[0, 2], [1, 256]], 0, -1, MASKED)
            select(m["band"][:, :, :], [[0, 2], [-1, 256]], P, 1, MASKED)
            select(m["causal"][:, :, :], [[0, 4], [1, P]], 0, -1, MASKED)
            inner = m["inner"][:, :].rearrange("p (b c) -> p b c", b=BATCH)
            select(inner, [[0, BATCH], [1, TPB]], 0, 1, 0.0, ALU.not_equal)

        @block.vector
        def _(dve):
            ones(nc.vector.memset(m["krep"][:, :, :, :], 1.0))
            split_biases(nc.vector, dve, m, Chain(ctx, nc, dve, "bias0_chain"), *bias)
            ones(nc.vector.memset(m["Vext"][:, :, :, :], 1.0))
            dve.wait_ge(ones.sem, 2)

        @block.sync
        def _(sp):
            n = 0
            load_biases(sp, m, A["L0_ffn_be1"], A["L0_ffn_be2"], bias[0])

            def load(dst, src):
                nonlocal n
                sp.dma_start(dst, src).then_inc(sem, 16)
                n += 1

            load(m["X"][:, :, :], A["L0_attn_hidden_states"].rearrange("b (c p) d -> p (b c) d", p=P))
            for i, w in enumerate(("Wq", "Wk", "Wv", "Wo")):
                load(m["Wraw"][:, i * D:(i + 1) * D], A["L0_attn_" + w])
            load(m["bqk"][:, 0:1], A["L0_attn_bq"].rearrange("(p o) -> p o", o=1))
            load(m["bqk"][:, 1:2], A["L0_attn_bk"].rearrange("(p o) -> p o", o=1))

            def row(dst, src):
                load(dst, src.rearrange("(o n) -> o n", o=1).to_broadcast([P, src.shape[0]]))

            row(m["bv"][:, :], A["L0_attn_bv"])
            row(m["bo"][:, :], A["L0_attn_bo"])
            place_biases(sp, m, 0, *bias)
            sp.wait_ge(sem, 16 * n)


def load_experts0(sp, A, m, sem):
    n = 0

    def load(dst, src):
        nonlocal n
        sp.dma_start(dst, src).then_inc(sem, 16)
        n += 16

    def row(dst, src):
        load(dst, src.rearrange("(o n) -> o n", o=1).to_broadcast([P, src.shape[0]]))

    row(m["br"][:, :], A["L0_ffn_br"])
    row(m["bs2"][:, :], A["L0_ffn_bs2"])
    load(m["Wr0"][:, :], A["L0_ffn_Wr"])
    load(m["Ws1"][:, :], A["L0_ffn_Ws1"])
    load(m["Ws2"][:, :, :], A["L0_ffn_Ws2"].rearrange("(c p) d -> p c d", p=P))
    for c in range(4):
        load(m["bs1"][:, c:c + 1], A["L0_ffn_bs1"][c * P:(c + 1) * P].rearrange("(p o) -> p o", o=1))
    load(m["We1"][:, :, :], A["L0_ffn_We1"].rearrange("e p h -> p e h"))
    load(m["We2"][:, :, :], A["L0_ffn_We2"].rearrange("e (c p) d -> p (e c) d", p=P))
    return n


def bias_signals(nc, ctx, l):
    return ctx.new(f"bias{l}_loaded"), Signal(ctx, nc, f"bias{l}_split"), ctx.new(f"bias{l}_moved")


def split_biases(v, dve, m, link, loaded, split, moved):
    dve.wait_ge(loaded, 32)
    for k in range(3):
        if k:
            link(v.tensor_tensor(m["be"][:, :], m["be"][:, :], m["be_parts"][:, k - 1, :], ALU.subtract))
        split(v.tensor_copy(m["be_parts"][:, k, :], m["be"][:, :]))
        dve.wait_ge(split.sem, k + 1)


def load_biases(sp, m, b_up, b_down, loaded):
    up = b_up.shape[1]
    sp.dma_start(m["be"][:, 0:up], b_up).then_inc(loaded, 16)
    sp.dma_start(m["be"][:, up:up + D], b_down).then_inc(loaded, 16)


def place_biases(sp, m, l, loaded, split, moved):
    for k in range(3):
        sp.wait_ge(split.sem, k + 1)
        sp.dma_start(m["bias3"][l][k:k + 1, :].rearrange("o (e w) -> o e w", e=m["be"].shape[0]),
                     m["be_parts"][:, k, :]).then_inc(moved, 16)
    sp.wait_ge(moved, 16 * 3)


def stage_project(nc, m, ctx):
    def sg(name):
        return Signal(ctx, nc, "proj_" + name)

    wT_ps, wT_sb, xT_ps, xT_sb = sg("wT_ps"), sg("wT_sb"), sg("xT_ps"), sg("xT_sb")
    q_ps, k_ps, v_ps = sg("q_ps"), sg("k_ps"), sg("v_ps")
    q_read, k_read, qk_split, v_sb = sg("q_read"), sg("k_read"), sg("qk_split"), sg("v_sb")
    spilled = [ctx.new(f"proj_spilled{b}") for b in range(BATCH)]
    m["replicated"] = [ctx.new(f"qk_replicated{b}") for b in range(BATCH)]
    bank = m["bank"]
    with nc.Block() as block:
        @block.tensor
        def _(pe):
            for i in range(4):
                last = nc.tensor.transpose(bank(7)[:, i * D:(i + 1) * D], m["Wraw"][:, i * D:(i + 1) * D], m["ident"][:, :])
            wT_ps(last)
            for b in range(BATCH):
                if b >= 2:
                    pe.wait_ge(xT_sb.sem, b - 1)
                for c in range(TPB):
                    last = nc.tensor.transpose(bank(b % 2)[:, c * P:(c + 1) * P], m["X"][:, b * TPB + c, :], m["ident"][:, :])
                xT_ps(last)
                if b == 0:
                    pe.wait_ge(wT_sb.sem, 1)
                pe.wait_ge(xT_sb.sem, b + 1)
                xT = m["XT"][:, b * SEQ:(b + 1) * SEQ]
                if b >= 1:
                    pe.wait_ge(q_read.sem, b)
                q_ps(nc.tensor.matmul(bank(2), lhsT=m["WT"][:, 0:D], rhs=xT, start=True, stop=True))
                if b >= 1:
                    pe.wait_ge(k_read.sem, b)
                k_ps(nc.tensor.matmul(bank(3), lhsT=m["WT"][:, D:2 * D], rhs=xT, start=True, stop=True))
                if b >= 1:
                    pe.wait_ge(v_sb.sem, 3 * b)
                for w in range(5):
                    lo, hi = max(0, P * w - HALF), min(SEQ, P * w + HALF)
                    out = (bank(4)[0:HALF, 384:512] if w == 0 else bank(5)[0:HALF, 0:P] if w == 4
                           else bank(4)[:, (w - 1) * P:w * P])
                    last = nc.tensor.matmul(out, lhsT=xT[:, lo:hi], rhs=m["WT"][:, 2 * D:3 * D], start=True, stop=True)
                v_ps(last)

        @block.scalar
        def _(act):
            act.wait_ge(wT_ps.sem, 1)
            wT_sb(nc.scalar.copy(m["WT"][:, :], bank(7)))
            for b in range(BATCH):
                act.wait_ge(xT_ps.sem, b + 1)
                xT_sb(nc.scalar.copy(m["XT"][:, b * SEQ:(b + 1) * SEQ], bank(b % 2)))

        @block.vector
        def _(dve):
            v = nc.vector
            link = Chain(ctx, nc, dve, "proj_chain")
            for b in range(BATCH):
                tok = slice(b * SEQ, (b + 1) * SEQ)
                for i, (ps, read, bk, parts) in enumerate(((q_ps, q_read, 2, m["q3"]), (k_ps, k_read, 3, m["k3"]))):
                    dve.wait_ge(ps.sem, b + 1)
                    if b >= 2:
                        dve.wait_ge(spilled[b - 2], 32)
                    parts = parts[:, b % 2]
                    link(v.tensor_scalar(parts[:, 0, :], bank(bk), m["bqk"][:, i:i + 1], None, ALU.add))
                    read(v.scalar_tensor_tensor(m["rest"][:, :], bank(bk), m["bqk"][:, i:i + 1], parts[:, 0, :],
                                                ALU.add, ALU.subtract))
                    dve.wait_ge(read.sem, b + 1)
                    link(v.tensor_copy(parts[:, 1, :], m["rest"][:, :]))
                    qk_split(v.tensor_tensor(parts[:, 2, :], m["rest"][:, :], parts[:, 1, :], ALU.subtract))
                    dve.wait_ge(qk_split.sem, 2 * b + i + 1)
                dve.wait_ge(v_ps.sem, b + 1)
                bv = m["bv"][:, :].rearrange("p (h d) -> p h d", h=HEADS)

                def take(dst, src, n):
                    for i in range(n):
                        last = v.tensor_tensor(dst(i), src(i), bv[0:dst(i).shape[0]], ALU.add)
                    v_sb(last)

                def hd(ap):
                    return ap.rearrange("p (h d) -> p h d", h=HEADS)

                take(lambda i: m["Vext"][:, 5 * b + 1 + i, :, 0:HD], lambda i: hd(bank(4)[:, i * P:(i + 1) * P]), 3)
                take(lambda i: m["Vext"][0:HALF, 5 * b, :, 0:HD], lambda i: hd(bank(4)[0:HALF, 384:512]), 1)
                take(lambda i: m["Vext"][0:HALF, 5 * b + 4, :, 0:HD], lambda i: hd(bank(5)[0:HALF, 0:P]), 1)

        @block.sync
        def _(sp):
            for b in range(BATCH):
                for i, parts in enumerate((m["q3"], m["k3"])):
                    sp.wait_ge(qk_split.sem, 2 * b + i + 1)
                    sp.dma_start(m["qk_dram"][i, b].rearrange("k p t -> p k t"), parts[:, b % 2, :, :]).then_inc(spilled[b], 16)
                if b == 0:
                    sp.wait_ge(spilled[0], 32)
                    replicate(sp, m, 0, m["replicated"][0])
            for b in range(1, BATCH):
                sp.wait_ge(spilled[b], 32)
            sp.wait_ge(m["replicated"][0], REP_INC)


REP_DMAS = 2 * len(Q_PARTS) * 2
REP_INC = 16 * REP_DMAS


def replicate(sp, m, b, sem):
    for i, (dst, which) in enumerate(((m["qrep"], Q_PARTS), (m["krep"], K_PARTS))):
        for odd in range(2):
            for r, part in enumerate(which):
                src = m["qk_dram"][i, b, part].rearrange("(g o d) t -> o d g t", o=2, d=HD)[odd]
                p0 = HALF * odd + HD * r
                sp.dma_start(dst[p0:p0 + HD, b % 2, :, :], src).then_inc(sem, 16)


def stage_attention(nc, m, ctx, A):
    def sg(name):
        return Signal(ctx, nc, "att_" + name)

    s_ps, s_max, mT_ps, m_split = sg("s_ps"), sg("s_max"), sg("mT_ps"), sg("m_split")
    t_ps, exped, masked, o_ps, ctx_sb = sg("t_ps"), sg("exped"), sg("masked"), sg("o_ps"), sg("ctx_sb")
    cT_ps, cT_sb, w_ps, r_sb, t_done = sg("cT_ps"), sg("cT_sb"), sg("w_ps"), sg("r_sb"), sg("t_done")
    oT_sb, oq_ps, clear = sg("oT_sb"), sg("oq_ps"), sg("clear")
    placed = ctx.new("att_max_placed")
    weights = ctx.new("layer0_weights_loaded")
    bank = m["bank"]
    QUADS = HEADS // 4
    units = []
    for b in range(BATCH):
        units += [("max", (b * TPB + j) * QUADS + q) for j in range(TPB) for q in range(QUADS)]
        units += [("prob", (b * 5 + w) * QUADS + q) for w in range(5) for q in range(QUADS)]
    number = {u: i for i, u in enumerate(units)}

    def pair_of_banks(kind, n):
        i = 2 * (number[kind, n] % 3)
        return m["PS"][:, i * 512:(i + 2) * 512].rearrange("p (o g c) -> p o g c", o=2, g=2)

    def slot(h):
        return 4 * (h // 4) + 2 * (h % 2) + h % 4 // 2

    with nc.Block() as block:
        @block.tensor
        def _(pe):
            def free(kind, n):
                i = number[kind, n]
                if i >= 3:
                    last_kind, last_n = units[i - 3]
                    pe.wait_ge((s_max if last_kind == "max" else exped).sem, last_n + 1)

            def maxima(b):
                if b >= 1:
                    pe.wait_ge(m["replicated"][b], REP_INC)
                for j in range(TPB):
                    c0 = HALF if j == 0 else 0
                    c1 = 192 if j == TPB - 1 else 256
                    k0 = P * j - HALF
                    for q in range(QUADS):
                        n = (b * TPB + j) * QUADS + q
                        free("max", n)
                        out = pair_of_banks("max", n)[:, :, :, c0:c1]
                        for o in range(2):
                            nc.tensor.matmul(out[:, o], lhsT=m["identb"][:, :], rhs=m["band"][:, :, c0:c1], start=True, stop=False,
                                             skip_group_check=True)
                        for g in range(2):
                            for o in range(2):
                                rows = slice(HALF * o, HALF * o + QK_ROWS)
                                last = nc.tensor.matmul(out[:, o, g], lhsT=m["qrep"][rows, b % 2, 2 * q + g, j * P:(j + 1) * P],
                                                        rhs=m["krep"][rows, b % 2, 2 * q + g, k0 + c0:k0 + c1],
                                                        start=False, stop=g == 1, skip_group_check=True)
                        s_ps(last)
                    pe.wait_ge(s_max.sem, n + 1)
                    if b >= 1 and j == 0:
                        pe.wait_ge(r_sb.sem, b * TPB)
                    if b * TPB + j >= 1:
                        pe.wait_ge(m_split.sem, b * TPB + j)
                    mT_ps(nc.tensor.transpose(bank(7)[0:HEADS, 384:512], m["mx"][:, (b * TPB + j) * HEADS:(b * TPB + j + 1) * HEADS],
                                              m["ident"][:, :]))

            def scores_t(b, w):
                k0, k1 = max(0, P * w - HALF), min(SEQ, P * w + HALF)
                q0, q1 = max(0, P * (w - 1)), min(SEQ, P * (w + 1))
                c0 = P if w == 0 else 0
                for quad in range(QUADS):
                    n = (b * 5 + w) * QUADS + quad
                    free("prob", n)
                    out = pair_of_banks("prob", n)
                    for g in range(2):
                        for o in range(2):
                            rows = slice(HALF * o, HALF * o + QK_ROWS + MAX_PARTS)
                            last = nc.tensor.matmul(out[0:k1 - k0, o, g, c0:c0 + q1 - q0],
                                                    lhsT=m["krep"][rows, b % 2, 2 * quad + g, k0:k1],
                                                    rhs=m["qrep"][rows, b % 2, 2 * quad + g, q0:q1],
                                                    start=True, stop=True)
                    t_ps(last)

            def values(b, j):
                n = b * TPB + j
                pe.wait_ge(masked.sem, (b * 5 + j + 2) * QUADS)
                if n >= 1:
                    pe.wait_ge(oT_sb.sem, n)
                else:
                    pe.wait_ge(clear.sem, 1)
                for h in range(HEADS):
                    out = bank(6)[32 * (h % 4):32 * (h % 4) + HD + 1, h // 4 * P:(h // 4 + 1) * P]
                    for i, w in enumerate((j, j + 1)):
                        keys = HALF if w in (0, 4) else P
                        c = P * (1 - i)
                        last = nc.tensor.matmul(out, lhsT=m["Vext"][0:keys, 5 * b + w, h, :],
                                                rhs=m["PT"][0:keys, (b * 5 + w) % 3, slot(h), c:c + P], start=i == 0, stop=i == 1)
                o_ps(last)

            def by_query(n):
                pe.wait_ge(oT_sb.sem, n + 1)
                if n >= 1:
                    pe.wait_ge(r_sb.sem, n)
                for g in range(4):
                    last = nc.tensor.transpose(bank(7)[:, g * P:(g + 1) * P], m["oT"][:, g * P:(g + 1) * P], m["ident"][:, :])
                oq_ps(last)

            def project(n):
                pe.wait_ge(ctx_sb.sem, n + 1)
                cT_ps(nc.tensor.transpose(bank(7)[:, 0:P], m["ctx"][:, n % 2, :], m["ident"][:, :]))
                pe.wait_ge(cT_sb.sem, n + 1)
                w_ps(nc.tensor.matmul(bank(7)[:, P:2 * P], lhsT=m["ctxT"][:, :], rhs=m["WT"][:, 3 * D:4 * D], start=True, stop=True))

            for b in range(BATCH):
                maxima(b)
                pe.wait_ge(placed, 16 * 6 * (b + 1))
                for w in range(7):
                    if w <= 4:
                        scores_t(b, w)
                    if w >= 3:
                        by_query(b * TPB + w - 3)
                    if 2 <= w <= 5:
                        values(b, w - 2)
                    if w >= 3:
                        project(b * TPB + w - 3)

        @block.vector
        def _(dve):
            v = nc.vector
            link = Chain(ctx, nc, dve, "att_chain")

            def reduce(b):
                for j in range(TPB):
                    c0 = HALF if j == 0 else 0
                    c1 = 192 if j == TPB - 1 else 256
                    for q in range(QUADS):
                        n = (b * TPB + j) * QUADS + q
                        dve.wait_ge(s_ps.sem, n + 1)
                        s_max(v.tensor_reduce(m["mx"][:, 4 * n:4 * n + 4].rearrange("p (g o) -> p o g", o=2),
                                              pair_of_banks("max", n)[:, :, :, c0:c1], AX, ALU.max))
                    dve.wait_ge(mT_ps.sem, b * TPB + j + 1)
                    if b >= 1 and j == 0:
                        dve.wait_ge(placed, 16 * 6 * b)
                    src, tok = bank(7)[0:HEADS, 384:512], slice(j * P, (j + 1) * P)
                    link(v.tensor_scalar(m["m3"][:, 0, tok], src, -1.0, None, ALU.mult))
                    link(v.scalar_tensor_tensor(m["mrest"][:, :], src, -1.0, m["m3"][:, 0, tok], ALU.mult, ALU.subtract))
                    link(v.tensor_copy(m["m3"][:, 1, tok], m["mrest"][:, :]))
                    m_split(v.tensor_tensor(m["m3"][:, 2, tok], m["mrest"][:, :], m["m3"][:, 1, tok], ALU.subtract))

            def normalise(n):
                dve.wait_ge(oq_ps.sem, n + 1)
                if n >= 2:
                    dve.wait_ge(cT_ps.sem, n - 1)
                o = bank(7).rearrange("p (h e) -> p h e", h=HEADS)
                link(v.reciprocal(m["rden"][:, :], o[:, :, HD]))
                ctx_sb(v.tensor_tensor(m["ctx"][:, n % 2, :].rearrange("p (h d) -> p h d", h=HEADS), o[:, :, 0:HD],
                                       bcast_last(m["rden"][:, :], HD), ALU.mult))

            def residual(n):
                dve.wait_ge(w_ps.sem, n + 1)
                link(v.tensor_tensor(m["R"][:, n, :], bank(7)[:, P:2 * P], m["bo"][:, :], ALU.add))
                r_sb(v.tensor_tensor(m["R"][:, n, :], m["R"][:, n, :], m["X"][:, n, :], ALU.add))

            clear(v.memset(bank(6), 0.0))
            for b in range(BATCH):
                reduce(b)
                for n in range(b * TPB, (b + 1) * TPB):
                    normalise(n)
                    residual(n)

        @block.scalar
        def _(act):
            def exps(b, w):
                keys = HALF if w in (0, 4) else P
                c0, c1 = (P if w == 0 else 0), (P if w == 4 else 2 * P)
                n = b * 5 + w
                if n >= 3:
                    pb, pw = divmod(n - 3, 5)
                    act.wait_ge(o_ps.sem, pb * TPB + min(pw + 1, TPB))
                for quad in range(QUADS):
                    g = n * QUADS + quad
                    act.wait_ge(t_ps.sem, g + 1)
                    exped(nc.scalar.activation(m["PT"][0:keys, n % 3, 4 * quad:4 * quad + 4, c0:c1].rearrange("p (o g) c -> p o g c", o=2), pair_of_banks("prob", g)[0:keys, :, :, c0:c1],
                                               ACT.Exp, scale=1.0 / math.sqrt(HD)))

            def ctxT(n):
                act.wait_ge(cT_ps.sem, n + 1)
                cT_sb(nc.scalar.copy(m["ctxT"][:, :], bank(7)[:, 0:P]))

            def oT(n):
                act.wait_ge(o_ps.sem, n + 1)
                if n >= 1:
                    act.wait_ge(oq_ps.sem, n)
                oT_sb(nc.scalar.copy(m["oT"][:, :], bank(6)))

            for b in range(BATCH):
                for w in range(7):
                    if w <= 4:
                        exps(b, w)
                    if 2 <= w <= 5:
                        oT(b * TPB + w - 2)
                    if w >= 3:
                        ctxT(b * TPB + w - 3)

        @block.gpsimd
        def _(pool):
            for b in range(BATCH):
                for w in range(5):
                    keys = HALF if w in (0, 4) else P
                    n = b * 5 + w
                    for quad in range(QUADS):
                        g = n * QUADS + quad
                        pool.wait_ge(exped.sem, g + 1)
                        t = m["PT"][0:keys, n % 3, 4 * quad:4 * quad + 4, :]
                        if w >= 1:
                            last = nc.gpsimd.affine_select(out=t[:, :, 0:P], in_=t[:, :, 0:P], compare_op=ALU.is_ge, fill=0.0,
                                                           base=0, pattern=[[0, 4], [1, P]], channel_multiplier=-1)
                        if w <= 3:
                            last = nc.gpsimd.affine_select(out=t[:, :, P:2 * P], in_=t[:, :, P:2 * P], compare_op=ALU.is_ge,
                                                           fill=0.0, base=HALF if w == 0 else 0,
                                                           pattern=[[0, 4], [-1, P]], channel_multiplier=1)
                        masked(last)

        @block.sync
        def _(sp):
            replicate(sp, m, 1, m["replicated"][1])
            for b in range(BATCH):
                sp.wait_ge(m_split.sem, TPB * (b + 1))
                for o in range(2):
                    for part in range(MAX_PARTS):
                        p = HALF * o + QK_ROWS + part
                        sp.dma_start(m["qrep"][p:p + 1, b % 2, :, :], m["m3"][o:HEADS:2, part, :]).then_inc(placed, 16)
                if 1 <= b <= 2:
                    sp.wait_ge(o_ps.sem, TPB * b)
                    replicate(sp, m, b + 1, m["replicated"][b + 1])
                if b == 0:
                    experts = load_experts0(sp, A, m, weights)
            sp.wait_ge(placed, 16 * 6 * BATCH)
            sp.wait_ge(weights, experts)


def stage_layernorm(nc, m, ctx, name, out_dram=None):
    stats, rooted, done, cent = (Signal(ctx, nc, name + s) for s in ("_stats", "_rooted", "_done", "_agg"))
    stored = ctx.new(name + "_stored")
    with nc.Block() as block:
        @block.vector
        def _(dve):
            v = nc.vector
            for n in range(TILES):
                cent(v.bn_stats(m["bn"][:, n, :], m["R"][:, n, :]))
            for n in range(TILES):
                dve.wait_ge(cent.sem, n + 1)
                last = cent(v.bn_aggr(m["mv"][:, n, :], m["bn"][:, n, :]))
            dve.wait_ge(cent.sem, 2 * TILES)
            stats(v.tensor_scalar(m["std"][:, :], m["mv"][:, :, 1], 1e-5, None, ALU.add))
            dve.wait_ge(rooted.sem, 1)
            stats(v.reciprocal(m["rstd"][:, :], m["root"][:, :]))
            dve.wait_ge(stats.sem, 2)
            for n in range(TILES):
                done(v.tensor_scalar(m["X"][:, n, :], m["R"][:, n, :], m["mv"][:, n, 0:1], m["rstd"][:, n:n + 1], ALU.subtract, ALU.mult))

        @block.scalar
        def _(act):
            act.wait_ge(stats.sem, 1)
            rooted(nc.scalar.activation(m["root"][:, :], m["std"][:, :], ACT.Sqrt))

        @block.sync
        def _(sp):
            if out_dram is not None:
                o = out_dram.rearrange("b (c p) d -> p (b c) d", p=P)
                for q in range(4):
                    sp.wait_ge(done.sem, 4 * (q + 1))
                    sp.dma_start(o[:, 4 * q:4 * q + 4, :], m["X"][:, 4 * q:4 * q + 4, :]).then_inc(stored, 16)
                sp.wait_ge(stored, 64)
            else:
                sp.wait_ge(done.sem, TILES)


def transpose_x(nc, pe, m, x_ps, x_sb, banks):
    for q in range(TILES // 4):
        if q >= 2:
            pe.wait_ge(x_sb.sem, q - 1)
        for c in range(4):
            last = nc.tensor.transpose(m["bank"](banks[q % 2])[:, c * P:(c + 1) * P], m["X"][:, 4 * q + c, :], m["ident"][:, :])
        x_ps(last)


def copy_xt(nc, act, m, x_ps, x_sb, banks):
    for q in range(TILES // 4):
        act.wait_ge(x_ps.sem, q + 1)
        x_sb(nc.scalar.copy(m["XT"][:, q * 512:(q + 1) * 512], m["bank"](banks[q % 2])))


def stage_router(nc, m, ctx, layer, E, tau, NT, Wr, br, shared):
    def sg(name):
        return Signal(ctx, nc, f"route{layer}_" + name)

    x_ps, x_sb, l_ps, picked, c_ps = sg("x_ps"), sg("x_sb"), sg("l_ps"), sg("picked"), sg("c_ps")
    gap, gexp, slots, zz = sg("gap"), sg("gexp"), sg("slots"), sg("zz")
    h_ps, h_act, h_sb, y_ps, y_sb = sg("h_ps"), sg("h_act"), sg("h_sb"), sg("y_ps"), sg("y_sb")
    spilled = ctx.new(f"route{layer}_spilled")
    KN = 2 * TILES
    oh_T, ohT_sb, i_ps = sg("oh_T"), sg("ohT_sb"), sg("i_ps")
    bank = m["bank"]

    def shared_up(dve, v, q):
        for c in range(2):
            dve.wait_ge(h_act.sem, 2 * q + c + 1)
            dve.wait_ge(h_ps.sem, 4 * q + 3 + c)
            if q >= 1:
                dve.wait_ge(y_ps.sem, q)
            h_sb(v.scalar_tensor_tensor(m["sh_act"][:, c, :], bank(4 + c), m["bs1"][:, c:c + 1], m["sh_gate"][:, c, :],
                                        ALU.add, ALU.mult))

    def v3(t):
        return t[:, 0:TILES * E].rearrange("p (t e) -> p t e", e=E)

    L, EQ, VAL, OH1, OH2, OFF = (v3(t) for t in m["rt"])
    iota_e = m["iota_e"][:, :, 0:E]
    with nc.Block() as block:
        @block.tensor
        def _(pe):
            transpose_x(nc, pe, m, x_ps, x_sb, (0, 1))
            if layer == 1:
                pe.wait_ge(m["load1"], m["load1_n"])
            for n in range(TILES):
                pe.wait_ge(x_sb.sem, n // 4 + 1)
                last = nc.tensor.matmul(bank(2)[:, n * E:(n + 1) * E], lhsT=m["XT"][:, n * P:(n + 1) * P], rhs=Wr[:, :],
                                        start=True, stop=True)
            l_ps(last)

            def inverse():
                pe.wait_ge(slots.sem, 1)
                for i in range(KN):
                    last = nc.tensor.matmul(bank(3)[:, 0:3 * NT], lhsT=m["lo_hot"][:, i, :],
                                            rhs=m["hi_hot"][:, i, :, 0:NT], start=i == 0, stop=i == KN - 1)
                i_ps(last)

            if not shared:
                pe.wait_ge(picked.sem, 1)
                nc.tensor.matmul(bank(2)[:, 0:TILES * E], lhsT=m["tri_strict"][:, :], rhs=m["rt"][1][:, 0:TILES * E], start=True, stop=True)
                c_ps(nc.tensor.matmul(bank(3)[:, 0:TILES * E], lhsT=m["ones"][:, :], rhs=m["rt"][1][:, 0:TILES * E], start=True, stop=True))
                for k in range(2):
                    for n in range(TILES):
                        g = (k * TILES + n) // 4
                        if n % 4 == 0 and g >= 4:
                            pe.wait_ge(ohT_sb.sem, g - 3)
                        last = nc.tensor.transpose(bank(4 + g % 4)[0:E, n % 4 * P:(n % 4 + 1) * P],
                                                   m["rt"][3 + k][:, n * E:(n + 1) * E], m["ident"][:, :])
                        if n % 4 == 3:
                            oh_T(last)
                inverse()
            else:
                for q in range(4):
                    for c in (2, 3, 0, 1):
                        if q >= 1:
                            if c >= 2:
                                pe.wait_ge(h_act.sem, 2 * (q - 1) + c - 1)
                            else:
                                pe.wait_ge(h_sb.sem, 2 * (q - 1) + c + 1)
                        h_ps(nc.tensor.matmul(bank(4 + c), lhsT=m["Ws1"][:, c * P:(c + 1) * P],
                                              rhs=m["XT"][:, q * 512:(q + 1) * 512], start=True, stop=True))
                    if q == 0:
                        pe.wait_ge(picked.sem, 1)
                        nc.tensor.matmul(bank(2)[:, 0:TILES * E], lhsT=m["tri_strict"][:, :], rhs=m["rt"][1][:, 0:TILES * E],
                                         start=True, stop=True)
                        c_ps(nc.tensor.matmul(bank(3)[:, 0:TILES * E], lhsT=m["ones"][:, :], rhs=m["rt"][1][:, 0:TILES * E],
                                              start=True, stop=True))
                    pe.wait_ge(h_sb.sem, 2 * (q + 1))
                    for c in range(4):
                        n = 4 * q + c
                        if n >= 4:
                            pe.wait_ge(y_sb.sem, n // 4)
                        for k in range(2):
                            last = nc.tensor.matmul(bank(q % 2)[:, c * P:(c + 1) * P],
                                                    lhsT=m["sh_act"][:, k, c * P:(c + 1) * P], rhs=m["Ws2"][:, k, :],
                                                    start=k == 0, stop=k == 1)
                    y_ps(last)
                    if q == 0:
                        inverse()

        @block.scalar
        def _(act):
            copy_xt(nc, act, m, x_ps, x_sb, (0, 1))
            if layer == 1:
                for g in range(8):
                    act.wait_ge(oh_T.sem, g + 1)
                    ohT_sb(nc.scalar.copy(m["ohT"][:, g * 512:(g + 1) * 512], bank(4 + g % 4)[0:E, :]))
            if shared:
                for q in range(4):
                    for c in (2, 3):
                        act.wait_ge(h_ps.sem, 4 * q + c - 1)
                        if q >= 1:
                            act.wait_ge(h_sb.sem, 2 * (q - 1) + c - 1)
                        h_act(nc.scalar.activation(m["sh_gate"][:, c - 2, :], bank(4 + c), ACT.Gelu, bias=m["bs1"][:, c:c + 1]))
            act.wait_ge(gap.sem, 1)
            gexp(nc.scalar.activation(m["gexp"][:, :], m["gap"][:, :], ACT.Exp, scale=1.0 / tau))

        @block.vector
        def _(dve):
            v = nc.vector
            link = Chain(ctx, nc, dve, f"route{layer}_chain")
            dve.wait_ge(l_ps.sem, 1)
            src = bank(2)[:, 0:TILES * E].rearrange("p (t e) -> p t e", e=E)
            if br is not None:
                link(v.tensor_tensor(L, src, bcast_mid(br[:, :], TILES), ALU.add))
            else:
                link(v.tensor_copy(L, src))
            for k, oh in enumerate((OH1, OH2)):
                top = m["top"][:, k, :]
                link(v.tensor_reduce(top, L, AX, ALU.max))
                link(v.tensor_tensor(EQ, L, bcast_last(top, E), ALU.is_equal))
                link(v.scalar_tensor_tensor(VAL, EQ, -100.0, iota_e, ALU.mult, ALU.add))
                link(v.tensor_reduce(m["first"][:, :], VAL, AX, ALU.min))
                link(v.tensor_tensor(oh, VAL, bcast_last(m["first"][:, :], E), ALU.is_equal))
                if k == 0:
                    link(v.scalar_tensor_tensor(L, OH1, -3.0e38, L, ALU.mult, ALU.add))
            picked(v.tensor_tensor(EQ, OH1, OH2, ALU.add))
            gap(v.tensor_tensor(m["gap"][:, :], m["top"][:, 1, :], m["top"][:, 0, :], ALU.subtract))
            if shared:
                shared_up(dve, v, 0)
            dve.wait_ge(c_ps.sem, 1)
            cum = bank(2)[:, 0:TILES * E].rearrange("p (t e) -> p t e", e=E)
            tot = bank(3)[:, 0:TILES * E].rearrange("p (t e) -> p t e", e=E)
            link(v.memset(OFF[:, 0, :], 0.0))
            for n in range(1, TILES):
                link(v.tensor_tensor(OFF[:, n, :], OFF[:, n - 1, :], tot[:, n - 1, :], ALU.add))
            link(v.tensor_tensor(m["cnt"][:, 0:E], OFF[:, TILES - 1, :], tot[:, TILES - 1, :], ALU.add))
            link(v.tensor_scalar(m["cnt"][:, 0:E], m["cnt"][:, 0:E], (P - 1) / 2.0, 1.0 / P, ALU.add, ALU.mult))
            link(v.tensor_scalar(m["cnt"][:, 0:E], m["cnt"][:, 0:E], ROUND_MAGIC, None, ALU.add))
            link(v.tensor_scalar(m["cnt"][:, 0:E], m["cnt"][:, 0:E], ROUND_MAGIC, None, ALU.subtract))
            link(v.memset(m["start"][:, 0:1], 0.0))
            for e in range(1, E):
                link(v.tensor_tensor(m["start"][:, e:e + 1], m["start"][:, e - 1:e], m["cnt"][:, e - 1:e], ALU.add))
            link(v.tensor_scalar(m["base"][:, 0:E], m["start"][:, 0:E], float(P), None, ALU.mult))
            link(v.tensor_tensor(OFF, OFF, bcast_mid(m["base"][:, 0:E], TILES), ALU.add))
            link(v.tensor_tensor(OFF, OFF, cum, ALU.add))
            for k, oh in enumerate((OH1, OH2)):
                link(v.tensor_tensor(VAL, OFF, oh, ALU.mult))
                link(v.tensor_reduce(m["posf"][:, k, :], VAL, AX, ALU.add))
            posf = m["posf"][:, :, :].rearrange("p k n -> p (k n)")
            hi = m["hi"][:, :]
            link(v.tensor_scalar(hi, posf, (P - 1) / -2.0, 1.0 / P, ALU.add, ALU.mult))
            link(v.tensor_scalar(hi, hi, ROUND_MAGIC, None, ALU.add))
            link(v.tensor_scalar(hi, hi, ROUND_MAGIC, None, ALU.subtract))
            link(v.scalar_tensor_tensor(posf, hi, -float(P), posf, ALU.mult, ALU.add))
            link.loose(v.tensor_tensor(m["lo_hot"][:, :, :], bcast_mid(m["iota_j"][:, 0:P], KN), bcast_last(posf, P), ALU.is_equal))
            hot = m["hi_hot"][:, :, :, 0:NT]
            link(v.tensor_tensor(hot[:, :, 0, :], bcast_mid(m["iota_j"][:, 0:NT], KN), bcast_last(hi, NT), ALU.is_equal))
            link.loose(v.tensor_tensor(hot[:, :, 1, :], hot[:, :, 0, :], bcast_last(m["iota_j"][:, 0:KN], NT), ALU.mult))
            slots(v.tensor_scalar(hot[:, :, 2, :], hot[:, :, 0, :], m["iota_p"][:, 0:1], None, ALU.mult))
            cmp = m["cmp"][0:1, 0:NT * E].rearrange("p (j e) -> p j e", e=E)
            link(v.tensor_tensor(cmp, bcast_mid(m["start"][0:1, 0:E], NT), bcast_last(m["iota_j"][0:1, 0:NT], E), ALU.is_le))
            link(v.tensor_reduce(m["eidf"][0:1, 0:NT], cmp, AX, ALU.add))
            link(v.tensor_scalar(m["eidf"][0:1, 0:NT], m["eidf"][0:1, 0:NT], 1.0, None, ALU.subtract))
            link(v.tensor_copy(m["eid"][0:1, 0:NT], m["eidf"][0:1, 0:NT]))
            dve.wait_ge(i_ps.sem, 1)
            used, number, row = (bank(3)[:, i * NT:(i + 1) * NT] for i in range(3))
            dst, pad = m["dst"][:, 0:NT], m["pad"][:, 0:NT]
            link(v.tensor_copy(dst, row))
            link(v.scalar_tensor_tensor(dst, number, float(P), dst, ALU.mult, ALU.add))
            link(v.tensor_scalar(pad, dst, float(TOK), -float(TOK), ALU.is_ge, ALU.mult))
            link(v.tensor_tensor(pad, pad, dst, ALU.add))
            link(v.tensor_copy(m["token"][:, 0:NT], pad))
            link(v.tensor_scalar(pad, used, -1.0, 1.0, ALU.mult, ALU.add))
            link(v.tensor_tensor(pad, pad, m["iota_slot"][:, 0:NT], ALU.mult))
            link(v.tensor_tensor(dst, dst, pad, ALU.add))
            link(v.tensor_copy(m["dest"][:, 0:NT], dst))
            if shared:
                for q in range(4):
                    if q >= 1:
                        shared_up(dve, v, q)
                    dve.wait_ge(y_ps.sem, q + 1)
                    dst = m["R"][:, 4 * q:4 * q + 4, :]
                    y_sb(v.tensor_tensor(dst, bank(q % 2).rearrange("p (t d) -> p t d", t=4), bcast_mid(m["bs2"][:, :], 4), ALU.add))
                    dve.wait_ge(y_sb.sem, q + 1)
                    link(v.tensor_tensor(dst, dst, m["X"][:, 4 * q:4 * q + 4, :], ALU.add))
            dve.wait_ge(gexp.sem, 1)
            link(v.tensor_scalar(m["w"][:, 0, :], m["gexp"][:, :], 1.0, None, ALU.add))
            link(v.reciprocal(m["w"][:, 0, :], m["w"][:, 0, :]))
            link(v.tensor_tensor(m["w"][:, 1, :], m["w"][:, 0, :], m["gexp"][:, :], ALU.mult))

        @block.sync
        def _(sp):
            sp.dma_start(m["x_dram"][layer].rearrange("(c p) d -> p c d", p=P), m["X"][:, :, :]).then_inc(spilled, 16)
            sp.wait_ge(spilled, 16)


class Tile:

    def __init__(self, c, it=None):
        self.c, self.it = c, it
        self.two, self.four = c % 2, c % 4
        self.v = c if it is None else it * 4 + c
        self.rounds = c // 4 if it is None else it + c // 4

    def plus(self, k):
        return Tile(self.c + k, self.it)

    def at_least(self, k):
        return self.it is not None or self.c >= k


def walk(eng, NT, step):
    for c in range(4):
        step(Tile(c))
    with eng.Fori(0, (NT - 8) // 4) as it:
        for c in range(4, 8):
            step(Tile(c, it))
    for c in range(NT - 4, NT):
        step(Tile(c))


def stage_experts(nc, m, ctx, layer, NT, HID, W1, W2, bias3, E):
    def sg(name):
        return Signal(ctx, nc, f"exp{layer}_" + name)

    x_ps, x_sb, g_ps, h_ps, gelu, act_sb = sg("x_ps"), sg("x_sb"), sg("g_ps"), sg("h_ps"), sg("gelu"), sg("act_sb")
    aT_ps, aT_sb, y_ps, y_sb = sg("aT_ps"), sg("aT_sb"), sg("y_ps"), sg("y_sb")
    loaded = [ctx.new(f"exp{layer}_loaded{i}") for i in range(4)]
    stored = [ctx.new(f"exp{layer}_stored{i}") for i in range(4)]
    bank = m["bank"]
    glu = layer == 0
    UP = 2 * HID if glu else HID
    WB = UP + D
    KC = HID // P
    act_done = act_sb if glu else gelu
    w1 = W1[:, :, :].rearrange("p e h -> p (e h)")
    w2 = W2[:, :, :].rearrange("p c d -> p (c d)")

    with nc.Block() as block:
        @block.gpsimd
        def _(pool):
            def gather(t):
                if t >= 4:
                    pool.wait_ge(x_ps.sem, t - 3)
                nc.gpsimd.indirect_dma_start(
                    out=m["xin"][:, t % 4, :], out_offset=None, in_=m["x_dram"][layer][:, :],
                    in_offset=bass.IndirectOffsetOnAxis(ap=m["token"][:, t:t + 1], axis=0)).then_inc(loaded[t % 4], 16)

            def scatter(t):
                pool.wait_ge(y_sb.sem, t + 1)
                nc.gpsimd.indirect_dma_start(
                    out=m["y_dram"][layer][:, :], out_offset=bass.IndirectOffsetOnAxis(ap=m["dest"][:, t:t + 1], axis=0),
                    in_=m["y_sb"][:, t % 4, :], in_offset=None).then_inc(stored[t % 4], 16)

            for t in range(4):
                gather(t)
            for t in range(NT):
                if t + 4 < NT:
                    gather(t + 4)
                scatter(t)
            for s in stored:
                pool.wait_ge(s, 16 * (NT // 4))

        @block.tensor
        def _(pe):
            known = {}

            def expert(t):
                key = (t.it is None, t.c)
                if key not in known:
                    known[key] = load_expert(t)
                return known[key]

            def load_expert(t):
                return pe.value_load(m["eid"][0:1, bass.ds(t.v, 1)], min_val=0, max_val=E - 1)

            def x_t(t):
                pe.wait_ge(loaded[t.four], (t.rounds + 1) * 16)
                if t.at_least(1):
                    pe.wait_ge(x_sb.sem, t.v)
                x_ps(nc.tensor.transpose(bank(0)[:, 0:P], m["xin"][:, t.four, :], m["ident"][:, :]))

            def up(t, e):
                pe.wait_ge(x_sb.sem, t.v + 1)
                if t.at_least(2):
                    pe.wait_ge(act_done.sem, t.v - 1)
                for i in range(UP // HID - 1, -1, -1):
                    out = bank(2 + 2 * i + t.two)[:, 0:HID]
                    nc.tensor.matmul(out, lhsT=m["ones3"][:, :], rhs=bias3[:, bass.ds(e * WB + i * HID, HID)], start=True, stop=False)
                    last = nc.tensor.matmul(out, lhsT=m["xTt"][:, t.two, :], rhs=w1[:, bass.ds(e * UP + i * HID, HID)],
                                            start=False, stop=True)
                    (g_ps if i else h_ps)(last)

            def act_t(t):
                pe.wait_ge(act_done.sem, t.v + 1)
                if t.at_least(2):
                    pe.wait_ge(aT_sb.sem, t.v - 1)
                for k in range(KC):
                    last = nc.tensor.transpose(bank(6 + t.two)[:, k * P:(k + 1) * P], m["act_sb"][:, t.two, k * P:(k + 1) * P],
                                               m["ident"][:, :])
                aT_ps(last)

            def down(t, e):
                pe.wait_ge(aT_sb.sem, t.v + 1)
                if t.at_least(1):
                    pe.wait_ge(y_sb.sem, t.v)
                out = bank(1)[:, 0:P]
                nc.tensor.matmul(out, lhsT=m["ones3"][:, :], rhs=bias3[:, bass.ds(e * WB + UP, D)], start=True, stop=False)
                for k in range(KC):
                    last = nc.tensor.matmul(out, lhsT=m["actT"][:, t.two, k * P:(k + 1) * P],
                                            rhs=w2[:, bass.ds(e * (KC * D) + k * D, D)], start=False, stop=k == KC - 1)
                y_ps(last)

            x_t(Tile(0))

            def step(t):
                if t.at_least(1):
                    act_t(t.plus(-1))
                if t.it is not None or t.c < NT - 1:
                    x_t(t.plus(1))
                up(t, expert(t))
                if t.at_least(1):
                    e_before = expert(t.plus(-1))
                if t.c + 1 not in ((4, NT) if t.it is None else (8,)):
                    expert(t.plus(1))
                if t.at_least(1):
                    down(t.plus(-1), e_before)

            walk(pe, NT, step)
            act_t(Tile(NT - 1))
            down(Tile(NT - 1), expert(Tile(NT - 1)))

        @block.scalar
        def _(act):
            def x_copy(t):
                act.wait_ge(x_ps.sem, t.v + 1)
                if t.at_least(2):
                    act.wait_ge(h_ps.sem, t.v - 1)
                x_sb(nc.scalar.copy(m["xTt"][:, t.two, :], bank(0)[:, 0:P]))

            def activate(t):
                act.wait_ge((g_ps if glu else h_ps).sem, t.v + 1)
                if glu:
                    if t.at_least(2):
                        act.wait_ge(act_sb.sem, t.v - 1)
                    gelu(nc.scalar.activation(m["gate"][:, t.two, 0:HID], bank(4 + t.two)[:, 0:HID], ACT.Gelu))
                else:
                    if t.at_least(2):
                        act.wait_ge(aT_ps.sem, t.v - 1)
                    gelu(nc.scalar.activation(m["act_sb"][:, t.two, 0:HID], bank(2 + t.two)[:, 0:HID], ACT.Gelu))

            def y_copy(t):
                act.wait_ge(y_ps.sem, t.v + 1)
                if t.at_least(4):
                    act.wait_ge(stored[t.four], t.rounds * 16)
                y_sb(nc.scalar.copy(m["y_sb"][:, t.four, :], bank(1)[:, 0:P]))

            x_copy(Tile(0))

            def step(t):
                if t.it is not None or t.c < NT - 1:
                    x_copy(t.plus(1))
                activate(t)
                if t.at_least(1):
                    y_copy(t.plus(-1))

            walk(act, NT, step)
            y_copy(Tile(NT - 1))

        @block.vector
        def _(dve):
            v = nc.vector

            def aT_copy(t):
                dve.wait_ge(aT_ps.sem, t.v + 1)
                if t.at_least(2):
                    dve.wait_ge(y_ps.sem, t.v - 1)
                aT_sb(v.tensor_copy(m["actT"][:, t.two, 0:HID], bank(6 + t.two)[:, 0:HID]))

            def multiply(t):
                dve.wait_ge(gelu.sem, t.v + 1)
                dve.wait_ge(h_ps.sem, t.v + 1)
                if t.at_least(2):
                    dve.wait_ge(aT_ps.sem, t.v - 1)
                act_sb(v.tensor_tensor(m["act_sb"][:, t.two, 0:HID], bank(2 + t.two)[:, 0:HID], m["gate"][:, t.two, 0:HID], ALU.mult))

            def step(t):
                if t.at_least(1):
                    aT_copy(t.plus(-1))
                if glu:
                    multiply(t)

            walk(dve, NT, step)
            aT_copy(Tile(NT - 1))


def stage_combine(nc, m, ctx, layer):
    loaded = [ctx.new(f"comb{layer}_loaded{i}") for i in range(8)]
    added, stats, rooted, gb_ps, gb_used = (Signal(ctx, nc, f"comb{layer}_" + x) for x in
                                            ("added", "stats", "rooted", "gb_ps", "gb_used"))
    bank = m["bank"]
    QUART = TILES // 4
    with nc.Block() as block:
        @block.sync
        def _(sp):
            for k in range(2):
                rows = m["y_dram"][layer][k * TOK:(k + 1) * TOK, :].rearrange("(c p) d -> p c d", p=P)
                for q in range(4):
                    tiles = slice(q * QUART, (q + 1) * QUART)
                    sp.dma_start(m["G"][k][:, tiles, :], rows[:, tiles, :]).then_inc(loaded[4 * k + q], 16)

        @block.vector
        def _(dve):
            v = nc.vector
            link = Chain(ctx, nc, dve, f"comb{layer}_chain")

            def arrived(k, n):
                if n % QUART == 0:
                    dve.wait_ge(loaded[4 * k + n // QUART], 16)

            if layer == 0:
                for k in range(2):
                    for n in range(TILES):
                        arrived(k, n)
                        ins = v.scalar_tensor_tensor(m["R"][:, n, :], m["G"][k][:, n, :], m["w"][:, k, n:n + 1], m["R"][:, n, :],
                                                     ALU.mult, ALU.add)
                        (added if k else link.loose)(ins)
                    if k == 0:
                        link.settle()
                dve.wait_ge(added.sem, TILES)
                return
            for k in range(2):
                for n in range(TILES):
                    arrived(k, n)
                    link.loose(v.tensor_tensor(m["G"][k][:, n, :], m["G"][k][:, n, :], m["X"][:, n, :], ALU.add))
            link.settle()
            for k in range(2):
                for n in range(TILES):
                    link.loose(v.bn_stats(m["bn2"][:, k * TILES + n, :], m["G"][k][:, n, :]))
            link.settle()
            for i in range(2 * TILES):
                link.loose(v.bn_aggr(m["mv2"][:, i, :], m["bn2"][:, i, :]))
            link.settle()
            stats(v.tensor_scalar(m["rstd2"][:, :], m["mv2"][:, :, 1], 1e-6, None, ALU.add))
            dve.wait_ge(rooted.sem, 1)
            link(v.reciprocal(m["rstd2"][:, :], m["rstd2"][:, :]))
            for i in range(2 * TILES):
                k, n = divmod(i, TILES)
                dve.wait_ge(gb_ps.sem, i + 1)
                gb = bank(i % 8)
                g = m["G"][k][:, n, :]
                link(v.scalar_tensor_tensor(g, g, m["mv2"][:, i, 0:1], gb[:, 0:D], ALU.subtract, ALU.mult))
                gb_used(v.scalar_tensor_tensor(g, g, m["rstd2"][:, i:i + 1], gb[:, D:2 * D], ALU.mult, ALU.add))
                dve.wait_ge(gb_used.sem, i + 1)
                base = m["R"] if k else m["X"]
                added(v.scalar_tensor_tensor(m["R"][:, n, :], g, m["w"][:, k, n:n + 1], base[:, n, :], ALU.mult, ALU.add))
                if i >= TILES - 1:
                    dve.wait_ge(added.sem, i - TILES + 2)
            dve.wait_ge(added.sem, 2 * TILES)

        if layer == 1:
            @block.scalar
            def _(act):
                act.wait_ge(stats.sem, 1)
                rooted(nc.scalar.activation(m["rstd2"][:, :], m["rstd2"][:, :], ACT.Sqrt))

            @block.tensor
            def _(pe):
                for i in range(2 * TILES):
                    if i >= 8:
                        pe.wait_ge(gb_used.sem, i - 7)
                    gb_ps(nc.tensor.matmul(bank(i % 8)[:, 0:2 * D], lhsT=m["ohT"][:, i * P:(i + 1) * P], rhs=m["gb"][:, :],
                                           start=True, stop=True))


INNER = 256
NH, HP = 4, 64
NS = 64
NANG = NS // 2
Z0, X0, B0, DT0, DA0, TR0, AN0, PROJ = 0, 256, 512, 640, 644, 648, 652, 684
TWO_PI = 2.0 * math.pi
PI_PARTS = [6.28125, 0.0019350051879882812, 3.019915e-07]


def stage_ssm_project(nc, m, ctx, A):
    def sg(name):
        return Signal(ctx, nc, "sp_" + name)

    x_ps, x_sb, a_ps, b_ps, a_sb, b_sb = sg("x_ps"), sg("x_sb"), sg("a_ps"), sg("b_ps"), sg("a_sb"), sg("b_sb")
    first = ctx.new("ssm_loads")
    m["load1"] = ctx.new("layer1_loads")
    bias = bias_signals(nc, ctx, 1)
    bank = m["bank"]
    with nc.Block() as block:
        @block.sync
        def _(sp):
            sp.dma_start(m["Win"][:, :], A["L1_attn_W_in"]).then_inc(first, 16)
            load_biases(sp, m, A["L1_ffn_b1"], A["L1_ffn_b2"], bias[0])
            sp.dma_start(m["Wout"][:, :, :], A["L1_attn_W_out"].rearrange("(c p) d -> p c d", p=P)).then_inc(first, 16)

            def row(dst, src):
                sp.dma_start(dst, src.rearrange("(o n) -> o n", o=1).to_broadcast([P, src.shape[0]])).then_inc(first, 16)

            row(m["dtb"][:, :], A["L1_attn_dt_bias"])
            row(m["Dp"][:, :], A["L1_attn_D_param"])
            row(m["lng"][:, 0, :], A["L1_attn_Bn_g"])
            row(m["lng"][:, 1, :], A["L1_attn_Cn_g"])
            row(m["lnb"][:, 0, :], A["L1_attn_Bn_b"])
            row(m["lnb"][:, 1, :], A["L1_attn_Cn_b"])
            for dst, src in ((m["Wr1"][:, :], A["L1_ffn_router_w"]),
                             (m["gb"][:, 0:D], A["L1_ffn_gamma"]), (m["gb"][:, D:2 * D], A["L1_ffn_beta"]),
                             (m["w1"][:, :, :], A["L1_ffn_w1"].rearrange("e p h -> p e h")),
                             (m["w2"][:, :, :], A["L1_ffn_w2"].rearrange("e (c p) d -> p (e c) d", p=P))):
                sp.dma_start(dst, src).then_inc(m["load1"], 16)
            m["load1_n"] = 16 * 5
            place_biases(sp, m, 1, *bias)
            sp.wait_ge(first, 16 * 8)

        @block.tensor
        def _(pe):
            transpose_x(nc, pe, m, x_ps, x_sb, (0, 1))
            pe.wait_ge(first, 16 * 8)
            for n in range(TILES):
                pe.wait_ge(x_sb.sem, n // 4 + 1)
                if n >= 2:
                    pe.wait_ge(a_sb.sem, n - 1)
                    pe.wait_ge(b_sb.sem, n - 1)
                xT = m["XT"][:, n * P:(n + 1) * P]
                a_ps(nc.tensor.matmul(bank(2 + n % 2), lhsT=xT, rhs=m["Win"][:, 0:512], start=True, stop=True))
                b_ps(nc.tensor.matmul(bank(4 + n % 2)[:, 0:PROJ - 512], lhsT=xT, rhs=m["Win"][:, 512:PROJ], start=True, stop=True))

        @block.scalar
        def _(act):
            copy_xt(nc, act, m, x_ps, x_sb, (0, 1))
            for n in range(TILES):
                act.wait_ge(a_ps.sem, n + 1)
                a_sb(nc.scalar.copy(m["PJ"][:, n, 0:512], bank(2 + n % 2)))

        @block.vector
        def _(dve):
            split_biases(nc.vector, dve, m, Chain(ctx, nc, dve, "bias1_chain"), *bias)
            for n in range(TILES):
                dve.wait_ge(b_ps.sem, n + 1)
                b_sb(nc.vector.tensor_copy(m["PJ"][:, n, 512:PROJ], bank(4 + n % 2)[:, 0:PROJ - 512]))
            dve.wait_ge(b_sb.sem, TILES)


def stage_ssm_gates(nc, m, ctx):
    def sg(name):
        return Signal(ctx, nc, "sg_" + name)

    to_act, from_act, to_pe, from_pe, rows = sg("to_act"), sg("from_act"), sg("to_pe"), sg("from_pe"), sg("rows")
    z_act, z_dve, normed = sg("z_act"), sg("z_dve"), sg("normed")
    shifted = ctx.new("sg_shifted")
    bank = m["bank"]
    PJ = m["PJ"]
    x4 = PJ[:, :, X0:B0]

    def rotate(e, link, last, k, tmp):
        pair = m["BC"][:, :, k, :].rearrange("p t (n two) -> p t n two", two=2)
        dst = m["BCt"][:, :, k, :].rearrange("p t (n two) -> p t n two", two=2)
        sin, cos = (m["ang"][:, i, :].rearrange("p (t n) -> p t n", n=NANG) for i in range(2))
        ev, od = pair[:, :, :, 0], pair[:, :, :, 1]
        link(e.tensor_tensor(dst[:, :, :, 0], ev, cos, ALU.mult))
        link(e.tensor_tensor(tmp, od, sin, ALU.mult))
        link(e.tensor_tensor(dst[:, :, :, 0], dst[:, :, :, 0], tmp, ALU.subtract))
        link(e.tensor_tensor(dst[:, :, :, 1], ev, sin, ALU.mult))
        link(e.tensor_tensor(tmp, od, cos, ALU.mult))
        last(e.tensor_tensor(dst[:, :, :, 1], dst[:, :, :, 1], tmp, ALU.add))

    with nc.Block() as block:
        @block.vector
        def _(dve):
            v = nc.vector
            link = Chain(ctx, nc, dve, "sg_chain")
            acts = [0]

            def act_turn(ins):
                to_act(ins)
                acts[0] += 1
                return acts[0]

            link(v.tensor_tensor(m["sp"][:, :, 0:NH], PJ[:, :, DT0:DA0], bcast_mid(m["dtb"][:, :], TILES), ALU.add))
            link(v.tensor_copy(m["sp"][:, :, NH:2 * NH], PJ[:, :, DA0:TR0]))
            link(v.tensor_scalar(m["sq"][:, :, :], m["sp"][:, :, :], -1.0, None, ALU.mult))
            act_turn(v.tensor_tensor(m["sq"][:, :, :], m["sq"][:, :, :], m["sp"][:, :, :], ALU.max))
            BCp = PJ[:, :, B0:DT0].rearrange("p t (k n) -> p t k n", k=2)

            def stat(ap):
                return ap[:, :, :].unsqueeze(3).to_broadcast([P, TILES, 2, NS])

            def gb(ap):
                return ap[:, :, :].unsqueeze(1).to_broadcast([P, TILES, 2, NS])

            link(v.tensor_reduce(m["mean"][:, :, :], BCp, AX, ALU.add))
            link(v.tensor_scalar(m["mean"][:, :, :], m["mean"][:, :, :], 1.0 / NS, None, ALU.mult))
            link(v.tensor_tensor(m["BC"][:, :, :, :], BCp, stat(m["mean"]), ALU.subtract))
            link(v.tensor_tensor(m["BCt"][:, :, :, :], m["BC"][:, :, :, :], m["BC"][:, :, :, :], ALU.mult))
            link(v.tensor_reduce(m["var"][:, :, :], m["BCt"][:, :, :, :], AX, ALU.add))
            dve.wait_ge(from_act.sem, 1)
            link(v.tensor_scalar(m["sq"][:, :, :], m["sq"][:, :, :], 1.0, None, ALU.add))
            act_turn(v.tensor_scalar(m["sp"][:, :, :], m["sp"][:, :, :], 0.0, None, ALU.max))
            dve.wait_ge(from_act.sem, 3)
            link(v.tensor_scalar(m["te"][:, :, :], m["te"][:, :, :], 1.0, None, ALU.add))
            link(v.reciprocal(m["te"][:, :, :], m["te"][:, :, :]))
            link(v.tensor_tensor(m["sp"][:, :, :], m["sp"][:, :, :], m["sq"][:, :, :], ALU.add))
            DT = m["sp"][:, :, 0:NH]
            link(v.tensor_scalar(m["adt"][:, :, :], m["sp"][:, :, NH:2 * NH], -1.0, -1e-4, ALU.mult, ALU.min))
            link(v.tensor_tensor(m["adt"][:, :, :], m["adt"][:, :, :], DT, ALU.mult))
            link(v.tensor_tensor(m["ca"][:, :, :], DT, m["te"][:, :, :], ALU.mult))
            link(v.tensor_tensor(m["cb"][:, :, :], DT, m["ca"][:, :, :], ALU.subtract))
            link(v.tensor_tensor(m["cb"][:, :, :], m["cb"][:, :, :], bcast_last(m["inner"][:, :], NH), ALU.mult))
            link(v.tensor_reduce(m["dtm"][:, :], DT, AX, ALU.add))
            link(v.tensor_scalar(m["dtm"][:, :], m["dtm"][:, :], 1.0 / NH, None, ALU.mult))
            link(v.tensor_tensor(m["av"][:, :, :], PJ[:, :, AN0:PROJ], bcast_last(m["dtm"][:, :], NANG), ALU.mult))
            av, before = (m[k][:, :, :].rearrange("p (b c) n -> p b c n", c=TPB) for k in ("av", "av_before"))
            link(v.memset(before[:, :, 0, :], 0.0))
            for c in range(1, TPB):
                ins = v.tensor_tensor(before[:, :, c, :], before[:, :, c - 1, :], av[:, :, c - 1, :], ALU.add)
                (to_pe if c == TPB - 1 else link)(ins)
            act_turn(v.tensor_scalar(m["var"][:, :, :], m["var"][:, :, :], 1.0 / NS, 1e-5, ALU.mult, ALU.add))
            dve.wait_ge(z_act.sem, 1)
            z_dve(v.tensor_scalar(m["sz"][:, :, :], m["sz"][:, :, :], 1.0, None, ALU.add))
            dve.wait_ge(from_pe.sem, 1)
            link(v.tensor_copy(m["Lc"][:, :, :], bank(1)[:, 0:TILES * NH].rearrange("p (t h) -> p t h", h=NH)))
            link(v.tensor_copy(m["Le"][:, :, :], bank(2)[:, 0:TILES * NH].rearrange("p (t h) -> p t h", h=NH)))
            act_turn(v.tensor_tensor(m["Ld"][:, :, :], m["Le"][:, :, :], m["Lc"][:, :, :], ALU.subtract))
            for k in range(2):
                r, t = m["ang"][:, k, :], m["turns"][:, :]
                link(v.tensor_copy(r, bank(0)))
                link(v.tensor_scalar(t, r, 1.0 / TWO_PI, 0.25 * k, ALU.mult, ALU.add))
                link(v.tensor_scalar(t, t, ROUND_MAGIC, None, ALU.add))
                link(v.tensor_scalar(t, t, ROUND_MAGIC, None, ALU.subtract))
                for c in PI_PARTS:
                    link(v.scalar_tensor_tensor(r, t, -c, r, ALU.mult, ALU.add))
                if k == 1:
                    link(v.tensor_scalar(r, r, math.pi / 2, None, ALU.add))
                act_turn(v.tensor_scalar(r, r, 3.1415925, -3.1415925, ALU.min, ALU.max))
            dve.wait_ge(from_act.sem, 4)
            link(v.reciprocal(m["var"][:, :, :], m["var"][:, :, :]))
            link(v.tensor_tensor(m["BC"][:, :, :, :], m["BC"][:, :, :, :], stat(m["var"]), ALU.mult))
            link(v.tensor_tensor(m["BC"][:, :, :, :], m["BC"][:, :, :, :], gb(m["lng"]), ALU.mult))
            normed(v.tensor_tensor(m["BC"][:, :, :, :], m["BC"][:, :, :, :], gb(m["lnb"]), ALU.add))
            dve.wait_ge(normed.sem, 1)
            dve.wait_ge(from_act.sem, 9)
            rotate(v, link, rows, 0, m["turns"][:, :].rearrange("p (t n) -> p t n", n=NANG))
            dve.wait_ge(rows.sem, 1)

        @block.gpsimd
        def _(pool):
            link = Chain(ctx, nc, pool, "sg_pool_chain")
            pool.wait_ge(z_act.sem, 2)
            link(nc.gpsimd.tensor_tensor(m["sz"][:, :, :], m["sz"][:, :, :], PJ[:, :, Z0:X0], ALU.mult))
            pool.wait_ge(normed.sem, 1)
            pool.wait_ge(from_act.sem, 9)
            rotate(nc.gpsimd, link, link, 1, m["av"][:, :, :])

        @block.scalar
        def _(act):
            s = nc.scalar
            z_link = Chain(ctx, nc, act, "sg_gate_chain")
            act.wait_ge(to_act.sem, 1)
            from_act(s.activation(m["sq"][:, :, :], m["sq"][:, :, :], ACT.Exp, scale=-1.0))
            act.wait_ge(to_act.sem, 2)
            from_act(s.activation(m["sq"][:, :, :], m["sq"][:, :, :], ACT.Ln))
            from_act(s.activation(m["te"][:, :, :], PJ[:, :, TR0:AN0], ACT.Exp, scale=-1.0))
            z_act(s.activation(m["sz"][:, :, :], PJ[:, :, Z0:X0], ACT.Exp, scale=-1.0))
            act.wait_ge(to_act.sem, 3)
            from_act(s.activation(m["var"][:, :, :], m["var"][:, :, :], ACT.Sqrt))
            act.wait_ge(to_act.sem, 4)
            from_act(s.activation(m["eL"][:, :, :], m["Lc"][:, :, :], ACT.Exp))
            from_act(s.activation(m["eE"][:, :, :], m["Le"][:, :, :], ACT.Exp))
            from_act(s.activation(m["eD"][:, :, :], m["Ld"][:, :, :], ACT.Exp))
            act.wait_ge(z_dve.sem, 1)
            z_link(s.activation(m["sz"][:, :, :], m["sz"][:, :, :], ACT.Ln))
            z_act(s.activation(m["sz"][:, :, :], m["sz"][:, :, :], ACT.Exp, scale=-1.0))
            for k in range(2):
                act.wait_ge(to_act.sem, 5 + k)
                from_act(s.activation(m["ang"][:, k, :], m["ang"][:, k, :], ACT.Sin))

        @block.tensor
        def _(pe):
            pe.wait_ge(to_pe.sem, 1)
            adt = m["adt"][:, :, :].rearrange("p t h -> p (t h)")
            nc.tensor.matmul(bank(1)[:, 0:TILES * NH], lhsT=m["tri"][:, :], rhs=adt, start=True, stop=True)
            nc.tensor.matmul(bank(2)[:, 0:TILES * NH], lhsT=m["ones"][:, :], rhs=adt, start=True, stop=True)
            for lhsT, rhs, start in ((m["tri"], m["av"], True), (m["ones"], m["av_before"], False)):
                last = nc.tensor.matmul(bank(0), lhsT=lhsT[:, :], rhs=rhs[:, :, :].rearrange("p t n -> p (t n)"),
                                        start=start, stop=not start)
            from_pe(last)

        @block.sync
        def _(sp):
            def shift(dst, src):
                sp.dma_start(dst[1:P, :, :], src[0:P - 1, :, :]).then_inc(shifted, 16)
                sp.dma_start(dst[0:1, 1:TILES, :], src[P - 1:P, 0:TILES - 1, :]).then_inc(shifted, 16)
                sp.dma_start(dst[0:1, 0:1, :], m["zeros"][0:1, 0:dst.shape[2]].unsqueeze(1)).then_inc(shifted, 16)

            shift(m["xsh"][:, :, :], x4)
            sp.wait_ge(rows.sem, 1)
            shift(m["Bsh"][:, :, :], m["BCt"][:, :, 0, :])
            sp.wait_ge(shifted, 16 * 6)


def stage_ssm_scan(nc, m, ctx):
    def sg(name):
        return Signal(ctx, nc, "ss_" + name)

    t_ps, t_sb, g_ps, l_in, l_ps, e_in, e_sb = (sg(x) for x in ("t_ps", "t_sb", "g_ps", "l_in", "l_ps", "e_in", "e_sb"))
    wgt, xab, xe, y_ps, i_ps, st_ps, st_sb, y_sb = (sg(x) for x in ("wgt", "xab", "xe", "y_ps", "i_ps", "st_ps", "st_sb", "y_sb"))
    yT_ps, yT_sb, o_ps, r_sb, xd = (sg(x) for x in ("yT_ps", "yT_sb", "o_ps", "r_sb", "xd"))
    bank = m["bank"]

    def h4(ap, n):
        return ap.rearrange("p (h x) -> p h x", h=NH) if n else ap

    with nc.Block() as block:
        @block.tensor
        def _(pe):
            def front(n):
                if n >= 1:
                    pe.wait_ge(t_sb.sem, n)
                for i, src in enumerate((m["BCt"][:, n, 0, :], m["Bsh"][:, n, :], m["BCt"][:, n, 1, :])):
                    last = nc.tensor.transpose(bank(0)[0:NS, i * P:(i + 1) * P], src, m["ident"][:, :])
                t_ps(last)
                pe.wait_ge(l_in.sem, n + 1)
                if n >= 2:
                    pe.wait_ge(e_in.sem, n - 1)
                nc.tensor.matmul(bank(2 + n % 2), lhsT=m["ones"][:, :], rhs=m["adtri"][:, n % 2, :, :].rearrange("p h t -> p (h t)"),
                                 start=True, stop=False)
                l_ps(nc.tensor.matmul(bank(2 + n % 2), lhsT=m["identb"][:, :], rhs=m["causal"][:, :, :].rearrange("p h t -> p (h t)"),
                                      start=False, stop=True))
                pe.wait_ge(t_sb.sem, n + 1)
                if n >= 1:
                    pe.wait_ge(wgt.sem, 2 * n)
                for i in range(2):
                    last = nc.tensor.matmul(bank(1)[:, i * P:(i + 1) * P], lhsT=m["BT"][:, n % 2, i, :], rhs=m["BT"][:, n % 2, 2, :],
                                            start=True, stop=True)
                g_ps(last)

            def back(n):
                pe.wait_ge(xe.sem, 2 * (n + 1))
                if n >= 1:
                    pe.wait_ge(st_sb.sem, n)
                out = bank(6)[0:NS, 0:INNER]
                nc.tensor.matmul(out, lhsT=m["BCt"][:, n, 0, :], rhs=m["xae"][:, n % 2, 0, :], start=True, stop=False)
                st_ps(nc.tensor.matmul(out, lhsT=m["Bsh"][:, n, :], rhs=m["xae"][:, n % 2, 1, :], start=False, stop=True))
                if n >= 2:
                    pe.wait_ge(y_sb.sem, n - 1)
                yb = bank(4 + n % 2)
                if n % TPB:
                    i_ps(nc.tensor.matmul(yb[:, INNER:2 * INNER], lhsT=m["BT"][:, n % 2, 2, :], rhs=m["H"][:, n % 2, :],
                                          start=True, stop=True))
                pe.wait_ge(wgt.sem, 2 * (n + 1))
                for h in range(NH):
                    for i in range(2):
                        last = nc.tensor.matmul(yb[:, h * HP:(h + 1) * HP], lhsT=m["W"][:, n % 2, i, h, :],
                                                rhs=m["xab"][:, n % 2, i, h * HP:(h + 1) * HP], start=i == 0, stop=i == 1)
                y_ps(last)

            def project(n):
                pe.wait_ge(y_sb.sem, n + 1)
                if n >= 1:
                    pe.wait_ge(r_sb.sem, n)
                for k in range(2):
                    last = nc.tensor.transpose(bank(7)[:, k * P:(k + 1) * P], m["yg"][:, n % 2, k * P:(k + 1) * P], m["ident"][:, :])
                yT_ps(last)
                pe.wait_ge(yT_sb.sem, n + 1)
                for k in range(2):
                    last = nc.tensor.matmul(bank(7)[:, 2 * P:3 * P], lhsT=m["yT"][:, k * P:(k + 1) * P], rhs=m["Wout"][:, k, :],
                                            start=k == 0, stop=k == 1)
                o_ps(last)

            front(0)
            for n in range(TILES):
                if n + 1 < TILES:
                    front(n + 1)
                back(n)
                if n >= 1:
                    project(n - 1)
            project(TILES - 1)

        @block.vector
        def _(dve):
            v = nc.vector
            link = Chain(ctx, nc, dve, "ss_chain")

            def exponents(n):
                dve.wait_ge(l_ps.sem, n + 1)
                if n >= 2:
                    dve.wait_ge(wgt.sem, 2 * (n - 1))
                e_in(v.tensor_tensor(m["Ex"][:, n % 2, :, :], bank(2 + n % 2).rearrange("p (h t) -> p h t", h=NH),
                                     bcast_last(m["Lc"][:, n, :], P), ALU.subtract))

            def weights(n):
                dve.wait_ge(g_ps.sem, n + 1)
                dve.wait_ge(e_sb.sem, n + 1)
                if n >= 2:
                    dve.wait_ge(y_ps.sem, n - 1)
                for i in range(2):
                    wgt(v.tensor_tensor(m["W"][:, n % 2, i, :, :], m["Ex"][:, n % 2, :, :], bcast_mid(bank(1)[:, i * P:(i + 1) * P], NH),
                                        ALU.mult))

            def state(n):
                dve.wait_ge(st_ps.sem, n + 1)
                src = bank(6)[0:NS, 0:INNER]
                dst = m["H"][:, (n + 1) % 2, :]
                if n % TPB == 0:
                    st_sb(v.tensor_copy(dst, src))
                else:
                    if n >= 2:
                        dve.wait_ge(i_ps.sem, (n - 1) - (n - 1) // TPB)
                    link(v.tensor_tensor(h4(dst, 1), h4(m["H"][:, n % 2, :], 1), bcast_last(m["eE"][0:NS, n, :], HP), ALU.mult))
                    st_sb(v.tensor_tensor(dst, dst, src, ALU.add))
                dve.wait_ge(st_sb.sem, n + 1)

            def output(n):
                dve.wait_ge(y_ps.sem, n + 1)
                yb = bank(4 + n % 2)
                y = m["yg"][:, n % 2, :]
                dve.wait_ge(xd.sem, n + 1)
                link(v.tensor_tensor(y, y, yb[:, 0:INNER], ALU.add))
                if n % TPB:
                    link(v.tensor_tensor(h4(m["inter"][:, :], 1), h4(yb[:, INNER:2 * INNER], 1), bcast_last(m["eL"][:, n, :], HP), ALU.mult))
                    link(v.tensor_tensor(y, y, m["inter"][:, :], ALU.add))
                y_sb(v.tensor_tensor(y, y, m["sz"][:, n, :], ALU.mult))

            def residual(n):
                dve.wait_ge(o_ps.sem, n + 1)
                r_sb(v.tensor_tensor(m["R"][:, n, :], bank(7)[:, 2 * P:3 * P], m["X"][:, n, :], ALU.add))

            exponents(0)
            for n in range(TILES):
                weights(n)
                if n + 1 < TILES:
                    exponents(n + 1)
                state(n)
                output(n)
                if n >= 1:
                    residual(n - 1)
            residual(TILES - 1)
            dve.wait_ge(r_sb.sem, TILES)

        @block.gpsimd
        def _(pool):
            link = Chain(ctx, nc, pool, "ss_pool_chain")

            def rows(n):
                if n >= 2:
                    pool.wait_ge(l_ps.sem, n - 1)
                l_in(nc.gpsimd.tensor_tensor(m["adtri"][:, n % 2, :, :], bcast_mid(m["tri"][:, :], NH), bcast_last(m["adt"][:, n, :], P), ALU.mult))

            def inputs(n):
                if n >= 2:
                    pool.wait_ge(y_ps.sem, n - 1)
                for i, (src, coef) in enumerate(((m["PJ"][:, n, X0:B0], m["ca"]), (m["xsh"][:, n, :], m["cb"]))):
                    link(nc.gpsimd.tensor_tensor(h4(m["xab"][:, n % 2, i, :], 1), h4(src, 1), bcast_last(coef[:, n, :], HP), ALU.mult))
                    ins = nc.gpsimd.tensor_tensor(h4(m["xae"][:, n % 2, i, :], 1), h4(m["xab"][:, n % 2, i, :], 1),
                                          bcast_last(m["eD"][:, n, :], HP), ALU.mult)
                    xe(ins)

            def skip(n):
                if n >= 2:
                    pool.wait_ge(yT_ps.sem, n - 1)
                xd(nc.gpsimd.tensor_tensor(h4(m["yg"][:, n % 2, :], 1), h4(m["PJ"][:, n, X0:B0], 1), bcast_last(m["Dp"][:, :], HP), ALU.mult))

            rows(0)
            inputs(0)
            for n in range(TILES):
                if n + 1 < TILES:
                    rows(n + 1)
                skip(n)
                if n + 1 < TILES:
                    inputs(n + 1)

        @block.scalar
        def _(act):
            def copies(n):
                act.wait_ge(t_ps.sem, n + 1)
                if n >= 2:
                    act.wait_ge(y_ps.sem, n - 1)
                    if (n - 2) % TPB:
                        act.wait_ge(i_ps.sem, (n - 2) - (n - 2) // TPB)
                t_sb(nc.scalar.copy(m["BT"][:, n % 2, :, :], bank(0)[0:NS, 0:3 * P].rearrange("p (k t) -> p k t", k=3)))

            def decays(n):
                act.wait_ge(e_in.sem, n + 1)
                e_sb(nc.scalar.activation(m["Ex"][:, n % 2, :, :], m["Ex"][:, n % 2, :, :], ACT.Exp))

            def yT(n):
                act.wait_ge(yT_ps.sem, n + 1)
                if n >= 1:
                    act.wait_ge(o_ps.sem, n)
                yT_sb(nc.scalar.copy(m["yT"][:, :], bank(7)[:, 0:2 * P]))

            copies(0)
            decays(0)
            for n in range(TILES):
                if n + 1 < TILES:
                    copies(n + 1)
                    decays(n + 1)
                if n >= 1:
                    yT(n - 1)
            yT(TILES - 1)


def build(nc, A, out, stop=99):
    NT0, NT1 = 44, 40
    m = {}
    top = ExitStack()
    with top:
        made = {}

        def alloc(scope, **shapes):
            for name, (shape, dt) in shapes.items():
                made[name] = made.get(name, 0) + 1
                m[name] = scope.enter_context(nc.sbuf_tensor(f"{name}_{made[name]}", shape, dt))

        sems = Semaphores(nc)
        m["PS"] = top.enter_context(nc.psum_tensor("banks", [P, 8 * 512], FP32))
        m["bank"] = lambda i: m["PS"][:, i * 512:(i + 1) * 512]
        alloc(top, ident=([P, P], FP32), identb=([P, P], BF16), tri=([P, P], FP32), tri_strict=([P, P], FP32),
              ones=([P, P], FP32), ones3=([3, P], BF16), band=([P, 2, 256], BF16), causal=([P, 4, P], BF16),
              zeros=([P, 256], FP32), inner=([P, TILES], FP32), iota_e=([P, TILES, 12], FP32), iota_j=([P, P], FP32), iota_p=([P, 1], FP32), iota_slot=([P, NT0], FP32),
              X=([P, TILES, D], FP32), R=([P, TILES, D], FP32),
              bn=([P, TILES, 6], FP32), mv=([P, TILES, 2], FP32), std=([P, TILES], FP32), root=([P, TILES], FP32),
              rstd=([P, TILES], FP32), flag=([1, 4], BF16),
              top=([P, 2, TILES], FP32), first=([P, TILES], FP32), gap=([P, TILES], FP32), gexp=([P, TILES], FP32),
              cnt=([P, 12], FP32), start=([P, 12], FP32), base=([P, 12], FP32), posf=([P, 2, TILES], FP32),
              w=([P, 2, TILES], FP32),
              eidf=([1, NT0], FP32), eid=([1, NT0], I32))
        m["x_dram"] = [nc.dram_tensor(f"token_rows{l}", [TOK, D], FP32, kind="Internal").ap() for l in range(2)]
        m["y_dram"] = [nc.dram_tensor(f"expert_rows{l}", [2 * TOK + nt * P, D], FP32, kind="Internal").ap()
                       for l, nt in enumerate((NT0, NT1))]
        m["qk_dram"] = nc.dram_tensor("qk_parts", [2, BATCH, 3, P, SEQ], BF16, kind="Internal").ap()
        m["bias3"] = [None, None]

        layer0 = ExitStack()
        with layer0:
            alloc(layer0, br=([P, 12], FP32), bs2=([P, D], FP32), Wr0=([P, 12], FP32), Ws1=([P, 512], FP32),
                  Ws2=([P, 2, D], FP32), bs1=([P, 4], FP32), We1=([P, 12, 768], FP32), We2=([P, 36, D], FP32))
            m["bias3"][0] = layer0.enter_context(nc.sbuf_tensor("bias3_0", [3, 12 * 896], BF16))
            with ExitStack() as att:
                alloc(att, WT=([P, 4 * D], FP32), bv=([P, D], FP32), bo=([P, D], FP32), Vext=([P, 20, HEADS, HD + 1], FP32),
                      qrep=([P, 2, 8, SEQ], BF16), krep=([P, 2, 8, SEQ], BF16))
                with ExitStack() as proj:
                    alloc(proj, Wraw=([P, 4 * D], FP32), bqk=([P, 2], FP32), q3=([P, 2, 3, SEQ], BF16), k3=([P, 2, 3, SEQ], BF16),
                          rest=([P, SEQ], FP32), XT=([P, TOK], FP32))
                    alloc(proj, be=([12, 896], FP32), be_parts=([12, 3, 896], BF16))
                    stage_begin(nc, m, sems, A)
                    stage_project(nc, m, sems)
                alloc(att, PT=([P, 3, HEADS, 256], FP32), mx=([P, TILES * HEADS], FP32), m3=([HEADS, 3, SEQ], BF16),
                      mrest=([HEADS, P], FP32), rden=([P, HEADS], FP32), ctx=([P, 2, D], FP32), ctxT=([P, D], FP32), oT=([P, 512], FP32))
                stage_attention(nc, m, sems, A)
            stage_layernorm(nc, m, sems, "ln0", out if stop == 0 else None)
            if stop == 0:
                return
            def tiles(scope):
                alloc(scope, XT=([P, TOK], FP32), xin=([P, 4, D], FP32), xTt=([P, 2, P], FP32), gate=([P, 2, 512], FP32), act_sb=([P, 2, 512], FP32),
                      actT=([P, 2, 512], FP32), y_sb=([P, 4, D], FP32))
                alloc(scope, cmp=([1, NT0 * 12], FP32), hi=([P, 2 * TILES], FP32), lo_hot=([P, 2 * TILES, P], BF16),
                      hi_hot=([P, 2 * TILES, 3, NT0], BF16), dst=([P, NT0], FP32), pad=([P, NT0], FP32), token=([P, NT0], I32),
                      dest=([P, NT0], I32))
                l = made["cmp"] - 1
                m["rt"] = [scope.enter_context(nc.sbuf_tensor(f"route{l}_tmp{i}", [P, TILES * 12], FP32)) for i in range(6)]
                m["G"] = [scope.enter_context(nc.sbuf_tensor(f"gathered{l}_{k}", [P, TILES, D], FP32)) for k in range(2)]

            with ExitStack() as moe:
                tiles(moe)
                alloc(moe, sh_gate=([P, 2, 512], FP32), sh_act=([P, 2, 512], FP32))
                stage_router(nc, m, sems, 0, 12, 1.5, NT0, m["Wr0"], m["br"], True)
                stage_experts(nc, m, sems, 0, NT0, 384, m["We1"], m["We2"], m["bias3"][0], 12)
                stage_combine(nc, m, sems, 0)
        stage_layernorm(nc, m, sems, "ln1", out if stop == 1 else None)
        if stop == 1:
            return
        sems.close()
        sems = Semaphores(nc)
        with ExitStack() as layer1:
            alloc(layer1, Wr1=([P, 8], FP32), w1=([P, 8, 512], FP32), w2=([P, 32, D], FP32), gb=([8, 2 * D], FP32))
            m["bias3"][1] = layer1.enter_context(nc.sbuf_tensor("bias3_1", [3, 8 * 640], BF16))
            with ExitStack() as ssm:
                alloc(ssm, Win=([P, PROJ], FP32), Wout=([P, 2, D], FP32), dtb=([P, NH], FP32), Dp=([P, NH], FP32),
                      lng=([P, 2, NS], FP32), lnb=([P, 2, NS], FP32), PJ=([P, TILES, PROJ], FP32), sz=([P, TILES, INNER], FP32),
                      adt=([P, TILES, NH], FP32), ca=([P, TILES, NH], FP32), cb=([P, TILES, NH], FP32), te=([P, TILES, NH], FP32),
                      Lc=([P, TILES, NH], FP32), Le=([P, TILES, NH], FP32), Ld=([P, TILES, NH], FP32),
                      eL=([P, TILES, NH], FP32), eE=([P, TILES, NH], FP32), eD=([P, TILES, NH], FP32),
                      BCt=([P, TILES, 2, NS], FP32), xsh=([P, TILES, INNER], FP32), Bsh=([P, TILES, NS], FP32))
                with ExitStack() as proj:
                    alloc(proj, XT=([P, TOK], FP32), be=([8, 640], FP32), be_parts=([8, 3, 640], BF16))
                    stage_ssm_project(nc, m, sems, A)
                with ExitStack() as gates:
                    alloc(gates, sp=([P, TILES, 8], FP32), sq=([P, TILES, 8], FP32), mean=([P, TILES, 2], FP32),
                          var=([P, TILES, 2], FP32), BC=([P, TILES, 2, NS], FP32), dtm=([P, TILES], FP32),
                          av=([P, TILES, NANG], FP32), av_before=([P, TILES, NANG], FP32), ang=([P, 2, TILES * NANG], FP32), turns=([P, TILES * NANG], FP32))
                    stage_ssm_gates(nc, m, sems)
                with ExitStack() as scan:
                    alloc(scan, adtri=([P, 2, NH, P], FP32), Ex=([P, 2, NH, P], FP32), W=([P, 2, 2, NH, P], FP32),
                          BT=([NS, 2, 3, P], FP32), xab=([P, 2, 2, INNER], FP32), xae=([P, 2, 2, INNER], FP32),
                          H=([NS, 2, INNER], FP32), yg=([P, 2, INNER], FP32), inter=([P, INNER], FP32), yT=([P, INNER], FP32))
                    stage_ssm_scan(nc, m, sems)
            stage_layernorm(nc, m, sems, "ln2", out if stop == 2 else None)
            if stop == 2:
                return
            with ExitStack() as moe:
                tiles(moe)
                alloc(moe, ohT=([8, 2 * TOK], FP32), bn2=([P, 2 * TILES, 6], FP32), mv2=([P, 2 * TILES, 2], FP32),
                      rstd2=([P, 2 * TILES], FP32))
                stage_router(nc, m, sems, 1, 8, 1.0, NT1, m["Wr1"], None, False)
                stage_experts(nc, m, sems, 1, NT1, 512, m["w1"], m["w2"], m["bias3"][1], 8)
                stage_combine(nc, m, sems, 1)
            stage_layernorm(nc, m, sems, "ln3", out)


def kernel(**inputs):
    import numpy as _np
    import concourse.bacc as _bacc
    from concourse import mybir as _mybir
    from concourse.bass_utils import run_bass_kernel_spmd as _run

    nc = _bacc.Bacc("TRN2", target_bir_lowering=False, num_devices=1)
    arrays, args = {}, {}
    for name in inputs:
        a = _np.ascontiguousarray(inputs[name])
        arrays[f"in_{name}"] = a
        args[name] = nc.dram_tensor(f"in_{name}", a.shape, _mybir.dt.from_np(a.dtype), kind="ExternalInput").ap()
    out = nc.dram_tensor("out_dram", (BATCH, SEQ, D), _mybir.dt.float32, kind="ExternalOutput").ap()
    build(nc, args, out)
    r = _run(nc, [arrays], core_ids=[0])
    return r.results[0]["out_dram"]
```
